# Optimizing a Trainium2 kernel written in Bass

```python
import numpy as np
import jax
import jax.numpy as jnp

def _softmax(x, axis=-1):
    return jax.nn.softmax(x, axis=axis)
def _gelu(x):
    return jax.nn.gelu(x, approximate=True)
def _silu(x):
    return jax.nn.silu(x)
def _sigmoid(x):
    return jax.nn.sigmoid(x)
def _layernorm(x, axis=-1, eps=1e-5):
    m = jnp.mean(x, axis=axis, keepdims=True)
    v = jnp.var(x, axis=axis, keepdims=True)
    return (x - m) / jnp.sqrt(v + eps)
def _scatter_add(tgt, idx, src, axis=0):
    return tgt.at[idx].add(src)
def _segment_sum(src, seg, n):
    return jax.ops.segment_sum(src, seg, n)

kernel_name = 'mk_conv_seq_d1_conv_nchw256_9c4d9e'

def setup_inputs(seed: int = 0):
    np.random.seed(seed)
    _w = jnp.asarray
    def _rec_inputs():
        import jax
        import jax.numpy as jnp
        _gk = jax.random.key(seed)
        x = -0.000125 + 0.9999 * jax.random.normal(jax.random.fold_in(_gk, 1), (32, 256, 64, 64), jnp.float32)
        return x
    x = _rec_inputs()
    def _L0_conv_setup():
        import jax, jax.numpy as jnp
        import numpy as np
        C = 256
        EPS = 1e-05

        def dwconv3x3(x, w):
            return jax.lax.conv_general_dilated(x, w, window_strides=(1, 1), padding=((1, 1), (1, 1)), dimension_numbers=('NCHW', 'OIHW', 'NCHW'), feature_group_count=x.shape[1])

        def bn(x, gamma, beta, mean, var):
            inv = gamma * jax.lax.rsqrt(var + EPS)
            return x * inv[:, None, None] + (beta - mean * inv)[:, None, None]
        key = jax.random.key(seed)
        ks = jax.random.split(key, 8)
        B, H, W = (32, 64, 64)
        inp = {'x': jax.random.normal(ks[0], (B, C, H, W), jnp.float32), 'edge_w': jax.random.normal(ks[1], (C, 1, 3, 3), jnp.float32) * 0.1, 'edge_gamma': jnp.ones((C,), jnp.float32), 'edge_beta': jnp.zeros((C,), jnp.float32), 'edge_mean': jnp.zeros((C,), jnp.float32), 'edge_var': jnp.ones((C,), jnp.float32), 'fc1_w': jax.random.normal(ks[2], (C // 16, C), jnp.float32) * 0.05, 'fc2_w': jax.random.normal(ks[3], (C, C // 16), jnp.float32) * 0.05, 'fusion_w': jax.random.normal(ks[4], (C, 2 * C), jnp.float32) * 0.05, 'fusion_b': jnp.zeros((C,), jnp.float32), 'bn1_gamma': jnp.ones((C,), jnp.float32), 'bn1_beta': jnp.zeros((C,), jnp.float32), 'bn1_mean': jnp.zeros((C,), jnp.float32), 'bn1_var': jnp.ones((C,), jnp.float32), 'deform_w': jax.random.normal(ks[5], (C, 1, 3, 3), jnp.float32) * 0.1, 'balance_w': jax.random.normal(ks[6], (C, C), jnp.float32) * 0.05, 'balance_b': jnp.zeros((C,), jnp.float32), 'bn2_gamma': jnp.ones((C,), jnp.float32), 'bn2_beta': jnp.zeros((C,), jnp.float32), 'bn2_mean': jnp.zeros((C,), jnp.float32), 'bn2_var': jnp.ones((C,), jnp.float32)}
        return inp
    _L0_conv_all = _L0_conv_setup()
    _L0_conv_in = {k: v for k, v in _L0_conv_all.items() if k in ('edge_w', 'edge_gamma', 'edge_beta', 'edge_mean', 'edge_var', 'fc1_w', 'fc2_w', 'fusion_w', 'fusion_b', 'bn1_gamma', 'bn1_beta', 'bn1_mean', 'bn1_var', 'deform_w', 'balance_w', 'balance_b', 'bn2_gamma', 'bn2_beta', 'bn2_mean', 'bn2_var', )}
    del _L0_conv_all

    return {
        "x": x,
        "L0_conv_edge_w": _L0_conv_in["edge_w"],
        "L0_conv_edge_gamma": _L0_conv_in["edge_gamma"],
        "L0_conv_edge_beta": _L0_conv_in["edge_beta"],
        "L0_conv_edge_mean": _L0_conv_in["edge_mean"],
        "L0_conv_edge_var": _L0_conv_in["edge_var"],
        "L0_conv_fc1_w": _L0_conv_in["fc1_w"],
        "L0_conv_fc2_w": _L0_conv_in["fc2_w"],
        "L0_conv_fusion_w": _L0_conv_in["fusion_w"],
        "L0_conv_fusion_b": _L0_conv_in["fusion_b"],
        "L0_conv_bn1_gamma": _L0_conv_in["bn1_gamma"],
        "L0_conv_bn1_beta": _L0_conv_in["bn1_beta"],
        "L0_conv_bn1_mean": _L0_conv_in["bn1_mean"],
        "L0_conv_bn1_var": _L0_conv_in["bn1_var"],
        "L0_conv_deform_w": _L0_conv_in["deform_w"],
        "L0_conv_balance_w": _L0_conv_in["balance_w"],
        "L0_conv_balance_b": _L0_conv_in["balance_b"],
        "L0_conv_bn2_gamma": _L0_conv_in["bn2_gamma"],
        "L0_conv_bn2_beta": _L0_conv_in["bn2_beta"],
        "L0_conv_bn2_mean": _L0_conv_in["bn2_mean"],
        "L0_conv_bn2_var": _L0_conv_in["bn2_var"],
    }

def reference(x, L0_conv_edge_w, L0_conv_edge_gamma, L0_conv_edge_beta, L0_conv_edge_mean, L0_conv_edge_var, L0_conv_fc1_w, L0_conv_fc2_w, L0_conv_fusion_w, L0_conv_fusion_b, L0_conv_bn1_gamma, L0_conv_bn1_beta, L0_conv_bn1_mean, L0_conv_bn1_var, L0_conv_deform_w, L0_conv_balance_w, L0_conv_balance_b, L0_conv_bn2_gamma, L0_conv_bn2_beta, L0_conv_bn2_mean, L0_conv_bn2_var):
    import jax
    import jax.numpy as jnp
    def _L0_conv_ref(x, edge_w, edge_gamma, edge_beta, edge_mean, edge_var, fc1_w, fc2_w, fusion_w, fusion_b, bn1_gamma, bn1_beta, bn1_mean, bn1_var, deform_w, balance_w, balance_b, bn2_gamma, bn2_beta, bn2_mean, bn2_var):
        import jax, jax.numpy as jnp
        import numpy as np
        C = 256
        EPS = 1e-05

        def dwconv3x3(x, w):
            return jax.lax.conv_general_dilated(x, w, window_strides=(1, 1), padding=((1, 1), (1, 1)), dimension_numbers=('NCHW', 'OIHW', 'NCHW'), feature_group_count=x.shape[1])

        def bn(x, gamma, beta, mean, var):
            inv = gamma * jax.lax.rsqrt(var + EPS)
            return x * inv[:, None, None] + (beta - mean * inv)[:, None, None]
        edge = jax.nn.relu(bn(dwconv3x3(x, edge_w), edge_gamma, edge_beta, edge_mean, edge_var))
        avg = jnp.mean(x, axis=(2, 3))
        att = jax.nn.relu(avg @ fc1_w.T)
        att = jax.nn.sigmoid(att @ fc2_w.T)
        enhanced = x * att[:, :, None, None]
        fused = jnp.concatenate([enhanced, edge], axis=1)
        out = jnp.einsum('bchw,oc->bohw', fused, fusion_w) + fusion_b[None, :, None, None]
        out = bn(out, bn1_gamma, bn1_beta, bn1_mean, bn1_var)
        out = dwconv3x3(out, deform_w)
        out = jnp.einsum('bchw,oc->bohw', out, balance_w) + balance_b[None, :, None, None]
        out = bn(out, bn2_gamma, bn2_beta, bn2_mean, bn2_var)
        return out * x

    def _gn(v, G=32, eps=1e-5):
        B_, C_, H_, W_ = v.shape
        g = v.reshape(B_, G, C_ // G, H_, W_)
        m = jnp.mean(g, axis=(2, 3, 4), keepdims=True)
        s = jnp.var(g, axis=(2, 3, 4), keepdims=True)
        return ((g - m) / jnp.sqrt(s + eps)).reshape(v.shape)

    def _ln_c(v, eps=1e-6):
        m = jnp.mean(v, axis=1, keepdims=True)
        s = jnp.var(v, axis=1, keepdims=True)
        return (v - m) / jnp.sqrt(s + eps)

    def _ln_t(v, eps=1e-5):
        m = jnp.mean(v, axis=-1, keepdims=True)
        s = jnp.var(v, axis=-1, keepdims=True)
        return (v - m) / jnp.sqrt(s + eps)

    def _to_tokens(v):
        B_, C_, H_, W_ = v.shape
        return v.reshape(B_, C_, H_ * W_).transpose(0, 2, 1)
    def _from_tokens(t, like):
        B_, C_, H_, W_ = like.shape
        return t.transpose(0, 2, 1).reshape(B_, C_, H_, W_)

    x = _L0_conv_ref(x, L0_conv_edge_w, L0_conv_edge_gamma, L0_conv_edge_beta, L0_conv_edge_mean, L0_conv_edge_var, L0_conv_fc1_w, L0_conv_fc2_w, L0_conv_fusion_w, L0_conv_fusion_b, L0_conv_bn1_gamma, L0_conv_bn1_beta, L0_conv_bn1_mean, L0_conv_bn1_var, L0_conv_deform_w, L0_conv_balance_w, L0_conv_balance_b, L0_conv_bn2_gamma, L0_conv_bn2_beta, L0_conv_bn2_mean, L0_conv_bn2_var)
    return x


_drawn_inputs = setup_inputs


def setup_inputs(seed=0):
    import zlib

    import numpy as np

    out = dict(_drawn_inputs(seed))
    spreads = {'L0_conv_edge_gamma': (1.0, 0.2),
     'L0_conv_edge_beta': (0.0, 0.1),
     'L0_conv_edge_mean': (0.0, 0.1),
     'L0_conv_edge_var': (1.0, 0.6),
     'L0_conv_fusion_b': (0.0, 0.1),
     'L0_conv_bn1_gamma': (1.0, 0.2),
     'L0_conv_bn1_beta': (0.0, 0.1),
     'L0_conv_bn1_mean': (0.0, 0.1),
     'L0_conv_bn1_var': (1.0, 0.2),
     'L0_conv_balance_b': (0.0, 0.1),
     'L0_conv_bn2_gamma': (1.0, 0.2),
     'L0_conv_bn2_beta': (0.0, 0.1),
     'L0_conv_bn2_mean': (0.0, 0.1),
     'L0_conv_bn2_var': (1.0, 0.2)}
    factors = {'L0_conv_fc1_w': 8.0, 'L0_conv_fc2_w': 8.0}
    for name, (base, spread) in spreads.items():
        noise = np.random.default_rng([zlib.crc32(name.encode()), seed]).standard_normal(out[name].shape)
        drawn = base * np.exp(spread * noise) if base else spread * noise
        out[name] = jnp.asarray(drawn.astype(out[name].dtype))
    for name, factor in factors.items():
        out[name] = (out[name] * factor).astype(out[name].dtype)
    return out
```

```python
import concourse.bass as bass
from concourse import mybir
from contextlib import ExitStack

IMAGES, CHANNELS, HEIGHT, WIDTH = 32, 256, 64, 64
P = 128
CHUNKS = CHANNELS // P
ROWS = 16
STRIPS = HEIGHT // ROWS
TOTAL = IMAGES * STRIPS
SIZE = ROWS * WIDTH
HALF = SIZE // 2
HALF_ROWS = ROWS // 2
RING = 2 * STRIPS
PAIRS = IMAGES // 2
PITCH = WIDTH + 1
HIDDEN = CHANNELS // 16
EPS = 1e-5

GAMMA, BETA, MEAN, VAR, BIAS, TAPS = 0, 6, 12, 18, 24, 28
PARAMS = TAPS + 2 * 9 * CHUNKS

PE_TAPS = [(0, 0), (0, -1), (0, 1), (1, -1), (1, 1)]
DVE_TAPS = [(-1, 0), (1, 0), (-1, -1), (-1, 1)]
CENTRE = (0, 0)
MIX_TAPS = [(dy, dx) for dy in (-1, 0, 1) for dx in (-1, 0, 1) if (dy, dx) != CENTRE]


def build(nc: bass.Bass, x, params, w1_t, w2_t, fc1_t, fc2_t, out):
    f32, f32r = mybir.dt.float32, mybir.dt.float32r
    ACT, ALU = mybir.ActivationFunctionType, mybir.AluOpType

    with ExitStack() as ctx:
        def sb(name, shape, dt=f32):
            return ctx.enter_context(nc.sbuf_tensor(name, shape, dt))

        def sem(name):
            return ctx.enter_context(nc.semaphore(name))

        xring = sb("xring", [P, 2, CHUNKS, HEIGHT * WIDTH])
        split_size = (ROWS + 1) * PITCH + 3
        xhi = sb("xhi", [P, 2, CHUNKS, split_size], f32r)
        xlo = sb("xlo", [P, 2, CHUNKS, split_size], f32r)
        mix_size = (HEIGHT + 2) * PITCH + 2
        mix = sb("mix", [P, CHUNKS, mix_size])
        edge = sb("edge", [P, SIZE])
        ehi = sb("ehi", [P, CHUNKS, SIZE], f32r)
        elo = sb("elo", [P, CHUNKS, SIZE], f32r)
        y = sb("y", [P, SIZE])
        yhi = sb("yhi", [P, CHUNKS, SIZE], f32r)
        ylo = sb("ylo", [P, CHUNKS, SIZE], f32r)
        gain = sb("gain", [P, CHUNKS, SIZE])
        w1x = sb("w1x", [P, CHUNKS, CHANNELS])
        w1x_hi = sb("w1x_hi", [P, CHUNKS, CHANNELS], f32r)
        w1x_lo = sb("w1x_lo", [P, CHUNKS, CHANNELS], f32r)
        w1e_hi = sb("w1e_hi", [P, CHUNKS, CHANNELS], f32r)
        w1e_lo = sb("w1e_lo", [P, CHUNKS, CHANNELS], f32r)
        w2_hi = sb("w2_hi", [P, CHUNKS, CHANNELS], f32r)
        w2_lo = sb("w2_lo", [P, CHUNKS, CHANNELS], f32r)
        diag_hi = sb("diag_hi", [P, len(PE_TAPS), CHUNKS, P], f32r)
        diag_lo = sb("diag_lo", [P, len(PE_TAPS), CHUNKS, P], f32r)
        prm = sb("prm", [P, PARAMS])
        tap_hi = sb("tap_hi", [P, 9 * CHUNKS], f32r)
        tap_lo = sb("tap_lo", [P, 9 * CHUNKS])
        bn = sb("bn", [P, 4, 6])
        fc1 = sb("fc1", [P, CHUNKS, HIDDEN])
        fc2 = sb("fc2", [HIDDEN, CHANNELS])
        sums = sb("sums", [P, 2, CHUNKS, STRIPS])
        hidden = sb("hidden", [HIDDEN, 1])
        att = sb("att", [P, CHUNKS])
        w1e_raw = gain[:, 0, 0:2 * CHANNELS].rearrange("p (k o) -> p k o", k=CHUNKS)
        w2_raw = gain[:, 0, 2 * CHANNELS:4 * CHANNELS].rearrange("p (k o) -> p k o", k=CHUNKS)
        ident = gain[:, 1, 0:P]

        acc1 = ctx.enter_context(nc.psum_tensor("acc1", [P, CHUNKS, SIZE], f32))
        acc2 = ctx.enter_context(nc.psum_tensor("acc2", [P, SIZE], f32))
        prod = ctx.enter_context(nc.psum_tensor("prod", [P, 2, HALF], f32))

        x_loaded = [sem(f"x_loaded{i}") for i in range(RING)]
        x_stored = [sem(f"x_stored{i}") for i in range(RING)]
        params_loaded, weights_loaded = sem("params_loaded"), sem("weights_loaded")
        pads_zeroed, ident_ready = sem("pads_zeroed"), sem("ident_ready")
        setup_step, root_ready = sem("setup_step"), sem("root_ready")
        his_ready, weights_ready = sem("his_ready"), sem("weights_ready")
        x_summed = sem("x_summed")
        xhi_ready, xlo_ready = sem("xhi_ready"), sem("xlo_ready")
        taps_on_pe = sem("taps_on_pe")
        acc1_tap = [sem(f"acc1_tap{c}") for c in range(CHUNKS)]
        edge_ready = sem("edge_ready")
        ehi_ready, elo_ready = sem("ehi_ready"), sem("elo_ready")
        w1_done, w2_done = sem("w1_done"), sem("w2_done")
        mix_ready = [sem(f"mix_ready{c}") for c in range(CHUNKS)]
        acc2_begun = sem("acc2_begun")
        acc2_tap = [sem(f"acc2_tap{c}") for c in range(CHUNKS)]
        yhi_ready, ylo_ready = sem("yhi_ready"), sem("ylo_ready")
        gain_ready = [sem(f"gain_ready{c}") for c in range(CHUNKS)]
        out_ready = sem("out_ready")
        fc1_done, hidden_ready = sem("fc1_done"), sem("hidden_ready")
        fc2_done, att_ready = sem("fc2_done"), sem("att_ready")
        w1x_hi_ready, w1x_lo_ready = sem("w1x_hi_ready"), sem("w1x_lo_ready")

        block = ctx.enter_context(nc.Block())

        def exists(pair, k):
            return not isinstance(pair, int) or 0 <= pair * RING + k < TOTAL

        def count(per_strip, pair, k, extra=0):
            return pair * (RING * per_strip) + (k * per_strip + extra)

        def image_count(per_image, pair, k, extra):
            return pair * (2 * per_image) + (k // STRIPS * per_image + extra)

        def turns(pair, k):
            return pair * 16 + 16 * (k // RING + 1)

        def first(k):
            return k % STRIPS == 0

        def last(k):
            return k % STRIPS == STRIPS - 1

        def tap_of(conv, tap, c):
            dy, dx = tap
            return TAPS + (conv * 9 + (dy + 1) * 3 + dx + 1) * CHUNKS + c

        def x_rows(k, c, row, rows, col=0, cols=WIDTH):
            at = (k % STRIPS) * ROWS + row
            image = xring[:, (k // STRIPS) % 2, c, at * WIDTH:(at + rows) * WIDTH]
            return image.rearrange("p (r w) -> p r w", w=WIDTH)[:, :, col:col + cols]

        def padded(row_tile, row, rows, dx=0):
            at = row * PITCH + 1 + dx
            return row_tile[:, at:at + rows * PITCH].rearrange("p (r w) -> p r w", w=PITCH)[:, :, 0:WIDTH]

        def written(row_tile, row, rows):
            return padded(row_tile, row, rows)

        def steps(eng, step):
            for k in range(-4, 4):
                step(0, k)
            with eng.Fori(0, PAIRS - 1) as pair:
                for k in range(4, 4 + RING):
                    step(pair, k)
            for k in range(4, 4 + RING):
                step(PAIRS - 1, k)

        x_pairs, out_pairs = (t.rearrange("(n i) (k p) h w -> n i p k (h w)", i=2, p=P) for t in (x, out))

        def load(sp, pair, slot):
            i, at = slot // STRIPS, (slot % STRIPS) * SIZE
            sp.dma_start(xring[:, i, :, at:at + SIZE], x_pairs[pair, i, :, :, at:at + SIZE]
                         ).then_inc(x_loaded[slot], 16)

        def store(sp, pair, slot):
            sp.wait_ge(out_ready, pair * (2 * RING) + (2 * slot + 2))
            i, at = slot // STRIPS, (slot % STRIPS) * SIZE
            sp.dma_start(out_pairs[pair, i, :, :, at:at + SIZE], xring[:, i, :, at:at + SIZE]
                         ).then_inc(x_stored[slot], 16)

        @block.sync
        def _(sp):
            load(sp, 0, 0)
            sp.dma_start(prm[:], params).then_inc(params_loaded, 16)
            sp.dma_start(w1x[:], w1_t[:, 0:CHUNKS, :]).then_inc(weights_loaded, 16)
            sp.dma_start(w1e_raw, w1_t[:, CHUNKS:2 * CHUNKS, :]).then_inc(weights_loaded, 16)
            sp.dma_start(w2_raw, w2_t).then_inc(weights_loaded, 16)
            sp.dma_start(fc1[:], fc1_t).then_inc(weights_loaded, 16)
            sp.dma_start(fc2[:], fc2_t).then_inc(weights_loaded, 16)
            for slot in range(1, RING):
                load(sp, 0, slot)
            with sp.Fori(0, PAIRS - 1) as pair:
                for slot in range(RING):
                    store(sp, pair, slot)
                    sp.wait_ge(x_stored[slot], pair * 16 + 16)
                    load(sp, pair + 1, slot)
            for slot in range(RING):
                store(sp, PAIRS - 1, slot)
            for slot in range(RING):
                sp.wait_ge(x_stored[slot], 16 * (PAIRS))

        @block.tensor
        def _(pe):
            pe.wait_ge(pads_zeroed, 1)
            pe.wait_ge(weights_ready, 1)

            def conv_taps(pair, k, c, half):
                buf = k % 2
                jobs = [(w, v) for w, v in ((diag_hi, xhi), (diag_lo, xhi), (diag_hi, xlo))]
                for job, (w, v) in enumerate(jobs):
                    if half == 0 and job == 0:
                        pe.wait_ge(xhi_ready, count(2, pair, k, c + 1))
                    if half == 0 and job == 2:
                        pe.wait_ge(xlo_ready, count(2, pair, k, c + 1))
                    for t, (dy, dx) in enumerate(PE_TAPS):
                        rows = HALF_ROWS - (last(k) and half == 1 and dy == 1)
                        at = half * HALF
                        mm = nc.tensor.matmul(
                            acc1[:, c, at:at + rows * WIDTH], w[:, t, c, :],
                            padded(v[:, buf, c, :], half * HALF_ROWS + dy, rows, dx),
                            start=(job == 0 and t == 0), stop=(job == 2 and t == len(PE_TAPS) - 1))
                return mm

            def step(pair, k):
                conv, image = exists(pair, k + 1), exists(pair, k) and first(k)
                strips = (pair, k + 1)
                for c in range(CHUNKS):
                    if conv:
                        if exists(pair, k):
                            pe.wait_ge(edge_ready, count(2, pair, k, c + 1))
                        conv_taps(*strips, c, 0)
                    if image and c == 0:
                        pe.wait_ge(x_summed, count(2, pair, k, 2 * STRIPS))
                        if exists(pair, k - 4):
                            pe.wait_ge(gain_ready[1], count(2, pair, k - 4, 1))
                        for n in range(CHUNKS * STRIPS):
                            cc, s = n // STRIPS, n % STRIPS
                            mm = nc.tensor.matmul(prod[0:HIDDEN, 0, 0:1], fc1[:, cc, :],
                                                  sums[:, (k // STRIPS) % 2, cc, s:s + 1],
                                                  start=(n == 0), stop=(n == CHUNKS * STRIPS - 1))
                        mm.then_inc(fc1_done, 1)
                    if conv:
                        conv_taps(*strips, c, 1).then_inc(taps_on_pe, 1)
                    if image and c == 0:
                        pe.wait_ge(hidden_ready, image_count(1, pair, k, 1))
                        if exists(pair, k - 4):
                            pe.wait_ge(gain_ready[1], count(2, pair, k - 4, 2))
                        for cc in range(CHUNKS):
                            mm = nc.tensor.matmul(prod[:, 1, cc:cc + 1], fc2[:, cc * P:(cc + 1) * P],
                                                  hidden[:], start=True, stop=True)
                        mm.then_inc(fc2_done, 1)

                if exists(pair, k):
                    buf = k % 2
                    for u in range(4):
                        o, half = u // 2, u % 2
                        if u == 0:
                            pe.wait_ge(w1x_hi_ready, image_count(2, pair, k, 2))
                            if exists(pair, k - 4):
                                pe.wait_ge(gain_ready[1], count(2, pair, k - 4, 1))
                        elif u == 1:
                            if exists(pair, k - 4):
                                pe.wait_ge(gain_ready[1], count(2, pair, k - 4, 2))
                        else:
                            pe.wait_ge(mix_ready[0], count(2, pair, k, u - 1))
                        jobs = []
                        for cc in range(CHUNKS):
                            v, l = (padded(b[:, buf, cc, :], half * HALF_ROWS, HALF_ROWS) for b in (xhi, xlo))
                            jobs += [(w1x_hi, cc, v, None), (w1x_hi, cc, l, None), (w1x_lo, cc, v, "att")]
                        for cc in range(CHUNKS):
                            v, l = (b[:, cc, half * HALF:(half + 1) * HALF] for b in (ehi, elo))
                            jobs += [(w1e_hi, cc, v, "ehi"), (w1e_lo, cc, v, None), (w1e_hi, cc, l, "elo")]
                        for n, (w, cc, v, needs) in enumerate(jobs):
                            if u == 0 and needs == "att":
                                pe.wait_ge(w1x_lo_ready, image_count(2, pair, k, cc + 1))
                            if u == 0 and needs == "ehi":
                                pe.wait_ge(ehi_ready, count(2, pair, k, cc + 1))
                            if u == 0 and needs == "elo":
                                pe.wait_ge(elo_ready, count(2, pair, k, cc + 1))
                            mm = nc.tensor.matmul(prod[:, u % 2, :], w[:, cc, o * P:(o + 1) * P], v,
                                                  start=(n == 0), stop=(n == len(jobs) - 1))
                        mm.then_inc(w1_done, 1)

                if exists(pair, k - 3):
                    for u in range(4):
                        o, half = u // 2, u % 2
                        if u < 2:
                            if exists(pair, k):
                                pe.wait_ge(mix_ready[1], count(2, pair, k, u + 1))
                            else:
                                pe.wait_ge(gain_ready[1], count(2, pair, k - 4, u + 1))
                        else:
                            pe.wait_ge(gain_ready[0], count(2, pair, k - 3, u - 1))
                        jobs = []
                        for cc in range(CHUNKS):
                            v, l = (b[:, cc, half * HALF:(half + 1) * HALF] for b in (yhi, ylo))
                            jobs += [(w2_hi, cc, v, "yhi"), (w2_lo, cc, v, None), (w2_hi, cc, l, "ylo")]
                        for n, (w, cc, v, needs) in enumerate(jobs):
                            if u == 0 and needs == "yhi":
                                pe.wait_ge(yhi_ready, count(2, pair, k - 3, cc + 1))
                            if u == 0 and needs == "ylo":
                                pe.wait_ge(ylo_ready, count(2, pair, k - 3, cc + 1))
                            mm = nc.tensor.matmul(prod[:, u % 2, :], w[:, cc, o * P:(o + 1) * P], v,
                                                  start=(n == 0), stop=(n == len(jobs) - 1))
                        mm.then_inc(w2_done, 1)

            steps(pe, step)

        @block.scalar
        def _(act):
            act.wait_ge(setup_step, 1)
            nc.scalar.activation(bn[:, 3, :], bn[:, 2, :], ACT.Sqrt).then_inc(root_ready, 1)
            act.wait_ge(weights_loaded, 5 * 16)
            nc.scalar.activation(w1e_hi[:], w1e_raw, ACT.Copy).then_inc(his_ready, 1)
            nc.scalar.activation(w2_hi[:], w2_raw, ACT.Copy).then_inc(his_ready, 1)
            act.wait_ge(params_loaded, 16)
            nc.scalar.activation(tap_hi[:], prm[:, TAPS:TAPS + 9 * CHUNKS], ACT.Copy).then_inc(his_ready, 1)
            act.wait_ge(pads_zeroed, 1)

            def sum_x(pair, k):
                act.wait_ge(x_loaded[k % RING], turns(pair, k))
                if exists(pair, k - 3):
                    act.wait_ge(ehi_ready, count(2, pair, k - 3, 1))
                    act.wait_ge(elo_ready, count(2, pair, k - 3, 1))
                for c in range(CHUNKS):
                    if exists(pair, k - 1) or c:
                        act.wait_ge(x_summed, count(2, pair, k, c))
                    nc.scalar.activation(edge[:].rearrange("p (r w) -> p r w", w=WIDTH),
                                         x_rows(k, c, 0, ROWS), ACT.Copy,
                                         accum_out=sums[:, (k // STRIPS) % 2, c, k % STRIPS:k % STRIPS + 1]
                                         ).then_inc(x_summed, 1)

            def round_x(pair, k, c):
                if c == 0:
                    act.wait_ge(x_loaded[k % RING], turns(pair, k))
                    if not last(k):
                        act.wait_ge(x_loaded[(k + 1) % RING], turns(pair, k + 1))
                    if exists(pair, k - 2):
                        act.wait_ge(w1_done, count(4, pair, k - 2, 4))
                rows = ROWS + (not last(k))
                nc.scalar.activation(written(xhi[:, k % 2, c, :], 0, rows), x_rows(k, c, 0, rows),
                                     ACT.Copy).then_inc(xhi_ready, 1)

            def edge_out(pair, k, c):
                act.wait_ge(acc1_tap[c], count(4, pair, k, 4))
                if exists(pair, k - 1) or c:
                    act.wait_ge(elo_ready, count(2, pair, k, c))
                    act.wait_ge(ehi_ready, count(2, pair, k, c))
                if exists(pair, k + 2 + c):
                    act.wait_ge(x_summed, count(2, pair, k + 2 + c, 2))
                if isinstance(pair, int) and pair == 0 and k == 0 and c == 0:
                    act.wait_ge(weights_ready, 1)
                nc.scalar.activation(edge[:], acc1[:, c, :], ACT.Relu, bias=bn[:, 1, c:c + 1],
                                     scale=bn[:, 0, c:c + 1]).then_inc(edge_ready, 1)

            def round_edge(pair, k, c):
                act.wait_ge(edge_ready, count(2, pair, k, c + 1))
                if exists(pair, k - 1):
                    act.wait_ge(w1_done, count(4, pair, k))
                nc.scalar.activation(ehi[:, c, :], edge[:], ACT.Copy).then_inc(ehi_ready, 1)

            def mix_out(pair, k, u):
                o, half = u // 2, u % 2
                act.wait_ge(w1_done, count(4, pair, k, u + 1))
                if exists(pair, k - 3):
                    act.wait_ge(acc2_tap[o], count(8, pair, k - 2))
                rows = written(mix[:, o, :], 1 + (k % STRIPS) * ROWS + half * HALF_ROWS, HALF_ROWS)
                nc.scalar.activation(rows, prod[:, u % 2, :].rearrange("p (r w) -> p r w", w=WIDTH),
                                     ACT.Identity, bias=bn[:, 1, 2 + o:3 + o],
                                     scale=bn[:, 0, 2 + o:3 + o]).then_inc(mix_ready[o], 1)

            def begin_acc2(pair, k, c):
                act.wait_ge(mix_ready[c], count(2, pair, k, 2))
                if c:
                    act.wait_ge(acc2_tap[0], count(8, pair, k, 8))
                elif exists(pair, k - 1):
                    act.wait_ge(acc2_tap[1], count(8, pair, k))
                at = tap_of(1, CENTRE, c)
                nc.scalar.activation(acc2[:].rearrange("p (r w) -> p r w", w=WIDTH),
                                     padded(mix[:, c, :], 1 + (k % STRIPS) * ROWS, ROWS),
                                     ACT.Copy, scale=prm[:, at:at + 1]).then_inc(acc2_begun, 1)

            def round_y(pair, k, c):
                act.wait_ge(acc2_tap[c], count(8, pair, k, 8))
                if exists(pair, k - 1):
                    act.wait_ge(w2_done, count(4, pair, k))
                nc.scalar.activation(yhi[:, c, :], y[:], ACT.Copy).then_inc(yhi_ready, 1)

            def gain_out(pair, k, u):
                o, half = u // 2, u % 2
                act.wait_ge(w2_done, count(4, pair, k, u + 1))
                if exists(pair, k - 1):
                    act.wait_ge(out_ready, count(2, pair, k - 1, o + 1))
                nc.scalar.activation(gain[:, o, half * HALF:(half + 1) * HALF], prod[:, u % 2, :],
                                     ACT.Identity, bias=bn[:, 1, 4 + o:5 + o],
                                     scale=bn[:, 0, 4 + o:5 + o]).then_inc(gain_ready[o], 1)

            def attend(pair, k):
                act.wait_ge(fc1_done, image_count(1, pair, k, 1))
                nc.scalar.activation(hidden[:], prod[0:HIDDEN, 0, 0:1], ACT.Relu,
                                     scale=1.0 / (HEIGHT * WIDTH)).then_inc(hidden_ready, 1)
                act.wait_ge(fc2_done, image_count(1, pair, k, 1))
                nc.scalar.activation(att[:], prod[:, 1, 0:CHUNKS], ACT.Sigmoid).then_inc(att_ready, 1)
                act.wait_ge(att_ready, image_count(1, pair, k, 1))
                if exists(pair, k - 1):
                    act.wait_ge(w1_done, count(4, pair, k))
                for c in range(CHUNKS):
                    nc.scalar.activation(w1x_hi[:, c, :], w1x[:, c, :], ACT.Copy,
                                         scale=att[:, c:c + 1]).then_inc(w1x_hi_ready, 1)

            def step(pair, k):
                if exists(pair, k - 2):
                    begin_acc2(pair, k - 2, 0)
                if exists(pair, k - 3):
                    round_y(pair, k - 3, 1)
                if exists(pair, k):
                    edge_out(pair, k, 1)
                    round_edge(pair, k, 1)
                    if first(k):
                        attend(pair, k)
                    mix_out(pair, k, 0)
                    mix_out(pair, k, 1)
                if exists(pair, k - 2):
                    begin_acc2(pair, k - 2, 1)
                if exists(pair, k):
                    mix_out(pair, k, 2)
                if exists(pair, k + 1):
                    edge_out(pair, k + 1, 0)
                if exists(pair, k):
                    mix_out(pair, k, 3)
                if exists(pair, k + 2):
                    round_x(pair, k + 2, 0)
                if exists(pair, k - 3):
                    gain_out(pair, k - 3, 0)
                if exists(pair, k + 1):
                    round_edge(pair, k + 1, 0)
                if exists(pair, k - 3):
                    gain_out(pair, k - 3, 1)
                if exists(pair, k + 2):
                    round_x(pair, k + 2, 1)
                if exists(pair, k - 3):
                    gain_out(pair, k - 3, 2)
                    gain_out(pair, k - 3, 3)
                if exists(pair, k - 2):
                    round_y(pair, k - 2, 0)
                if exists(pair, k + 4):
                    sum_x(pair, k + 4)

            steps(act, step)

        @block.vector
        def _(dve):
            made = [0]

            def link(ins):
                made[0] += 1
                ins.then_inc(setup_step, 1)
                dve.wait_ge(setup_step, made[0])

            scale, shift, v, r = (bn[:, n, :] for n in range(4))
            t = y[:, 0:6]
            dve.wait_ge(params_loaded, 16)
            link(nc.vector.tensor_scalar(v, prm[:, VAR:VAR + 6], EPS, None, ALU.add))
            link(nc.vector.tensor_tensor(prm[:, MEAN + 2:MEAN + 6], prm[:, MEAN + 2:MEAN + 6],
                                         prm[:, BIAS:BIAS + 4], ALU.subtract))
            dve.wait_ge(root_ready, 1)
            link(nc.vector.reciprocal(r, r))
            link(nc.vector.tensor_tensor(t, r, r, ALU.mult))
            link(nc.vector.tensor_tensor(t, t, v, ALU.mult))
            link(nc.vector.tensor_scalar(t, t, -0.5, 1.5, ALU.mult, ALU.add))
            link(nc.vector.tensor_tensor(r, r, t, ALU.mult))
            link(nc.vector.tensor_tensor(scale, r, prm[:, GAMMA:GAMMA + 6], ALU.mult))
            link(nc.vector.tensor_tensor(t, scale, prm[:, MEAN:MEAN + 6], ALU.mult))
            link(nc.vector.tensor_tensor(shift, prm[:, BETA:BETA + 6], t, ALU.subtract))
            dve.wait_ge(his_ready, 3)
            nc.vector.tensor_tensor(w1e_lo[:], w1e_raw, w1e_hi[:].bitcast(f32), ALU.subtract)
            nc.vector.tensor_tensor(w2_lo[:], w2_raw, w2_hi[:].bitcast(f32), ALU.subtract)
            link(nc.vector.tensor_tensor(tap_lo[:], prm[:, TAPS:TAPS + 9 * CHUNKS], tap_hi[:].bitcast(f32),
                                         ALU.subtract))
            dve.wait_ge(ident_ready, 2)
            for n, tap in enumerate(PE_TAPS):
                for c in range(CHUNKS):
                    at = tap_of(0, tap, c) - TAPS
                    nc.vector.tensor_scalar(diag_hi[:, n, c, :], ident, tap_hi[:, at:at + 1].bitcast(f32),
                                            None, ALU.mult)
                    made_last = nc.vector.tensor_scalar(diag_lo[:, n, c, :], ident, tap_lo[:, at:at + 1],
                                                        None, ALU.mult)
            made_last.then_inc(weights_ready, 1)

            def acc1_op(pair, k, c, n):
                if n == 0:
                    dve.wait_ge(taps_on_pe, count(2, pair, k, c + 1))
                else:
                    dve.wait_ge(acc1_tap[c], count(4, pair, k, n))
                dy, dx = DVE_TAPS[n]
                top = 1 if first(k) and dy < 0 else 0
                rows = ROWS - top - (1 if last(k) and dy > 0 else 0)
                col, cols = max(0, -dx), WIDTH - abs(dx)
                acc = acc1[:, c, top * WIDTH:(top + rows) * WIDTH].rearrange("p (r w) -> p r w", w=WIDTH)
                acc = acc[:, :, col:col + cols]
                at = tap_of(0, (dy, dx), c)
                nc.vector.scalar_tensor_tensor(
                    out=acc, in0=x_rows(k, c, top + dy, rows, col + dx, cols), scalar=prm[:, at:at + 1],
                    in1=acc, op0=ALU.mult, op1=ALU.add).then_inc(acc1_tap[c], 1)

            def acc2_op(pair, k, c, n):
                if n == 0:
                    dve.wait_ge(acc2_begun, count(2, pair, k, c + 1))
                    if not last(k):
                        dve.wait_ge(mix_ready[c], count(2, pair, k + 1, 1))
                else:
                    dve.wait_ge(acc2_tap[c], count(8, pair, k, n))
                final = n == len(MIX_TAPS) - 1
                if final and (c or exists(pair, k - 1)):
                    dve.wait_ge(yhi_ready, count(2, pair, k, c))
                    dve.wait_ge(ylo_ready, count(2, pair, k, c))
                acc = acc2[:].rearrange("p (r w) -> p r w", w=WIDTH)
                to = y[:].rearrange("p (r w) -> p r w", w=WIDTH) if final else acc
                dy, dx = MIX_TAPS[n]
                at = tap_of(1, (dy, dx), c)
                nc.vector.scalar_tensor_tensor(
                    out=to, in0=padded(mix[:, c, :], 1 + (k % STRIPS) * ROWS + dy, ROWS, dx),
                    scalar=prm[:, at:at + 1], in1=acc, op0=ALU.mult, op1=ALU.add).then_inc(acc2_tap[c], 1)

            def step(pair, k):
                for c in range(CHUNKS):
                    taps = {1: 0, 2: 0}
                    for n, conv in enumerate((1, 2, 2, 1, 2, 2, 1, 2, 2, 2, 2, 1)):
                        if conv == 1 and exists(pair, k + 1):
                            acc1_op(pair, k + 1, c, taps[1])
                        if conv == 2 and exists(pair, k - 2):
                            acc2_op(pair, k - 2, c, taps[2])
                        taps[conv] += 1
                        if c == 0 and n == 3 and exists(pair, k) and first(k):
                            for cc in range(CHUNKS):
                                dve.wait_ge(w1x_hi_ready, image_count(2, pair, k, cc + 1))
                                nc.vector.scalar_tensor_tensor(
                                    out=w1x_lo[:, cc, :], in0=w1x[:, cc, :], scalar=att[:, cc:cc + 1],
                                    in1=w1x_hi[:, cc, :].bitcast(f32), op0=ALU.mult,
                                    op1=ALU.subtract).then_inc(w1x_lo_ready, 1)

            steps(dve, step)

        @block.gpsimd
        def _(pool):
            pool.memset(ident, 0.0).then_inc(ident_ready, 1)
            pool.wait_ge(ident_ready, 1)
            pool.affine_select(out=ident, in_=ident, compare_op=ALU.not_equal, fill=1.0, base=0,
                               pattern=[[-1, P]], channel_multiplier=1).then_inc(ident_ready, 1)
            for c in range(CHUNKS):
                for buf in range(2):
                    for tile in (xhi, xlo):
                        pool.memset(tile[:, buf, c, 0:(ROWS + 1) * PITCH + 1:PITCH].bitcast(f32), 0.0)
                pool.memset(mix[:, c, 0:PITCH + 1], 0.0)
                pool.memset(mix[:, c, 2 * PITCH:(HEIGHT + 1) * PITCH:PITCH], 0.0)
                zeroed = pool.memset(mix[:, c, (HEIGHT + 1) * PITCH:mix_size], 0.0)
            zeroed.then_inc(pads_zeroed, 1)

            def rest_of_x(pair, k, c):
                pool.wait_ge(xhi_ready, count(2, pair, k, c + 1))
                rows = ROWS + (not last(k))
                nc.gpsimd.tensor_tensor(written(xlo[:, k % 2, c, :], 0, rows), x_rows(k, c, 0, rows),
                                        written(xhi[:, k % 2, c, :], 0, rows).bitcast(f32), ALU.subtract
                                        ).then_inc(xlo_ready, 1)

            def rest_of_edge(pair, k, c):
                pool.wait_ge(ehi_ready, count(2, pair, k, c + 1))
                nc.gpsimd.tensor_tensor(elo[:, c, :], edge[:], ehi[:, c, :].bitcast(f32), ALU.subtract
                                        ).then_inc(elo_ready, 1)

            def rest_of_y(pair, k, c):
                pool.wait_ge(yhi_ready, count(2, pair, k, c + 1))
                nc.gpsimd.tensor_tensor(ylo[:, c, :], y[:], yhi[:, c, :].bitcast(f32), ALU.subtract
                                        ).then_inc(ylo_ready, 1)

            def times_x(pair, k, c):
                pool.wait_ge(gain_ready[c], count(2, pair, k, 2))
                at = (k % STRIPS) * SIZE
                strip = xring[:, (k // STRIPS) % 2, c, at:at + SIZE]
                nc.gpsimd.tensor_tensor(strip, strip, gain[:, c, :], ALU.mult).then_inc(out_ready, 1)

            def step(pair, k):
                if exists(pair, k - 3):
                    rest_of_y(pair, k - 3, 1)
                if exists(pair, k):
                    rest_of_edge(pair, k, 1)
                if exists(pair, k + 2):
                    rest_of_x(pair, k + 2, 0)
                if exists(pair, k + 1):
                    rest_of_edge(pair, k + 1, 0)
                if exists(pair, k + 2):
                    rest_of_x(pair, k + 2, 1)
                if exists(pair, k - 2):
                    rest_of_y(pair, k - 2, 0)
                if exists(pair, k - 3):
                    times_x(pair, k - 3, 0)
                    times_x(pair, k - 3, 1)

            steps(pool, step)


def kernel(**inputs):
    import numpy as _np
    import concourse.bacc as _bacc
    from concourse import mybir as _mybir
    from concourse.bass_utils import run_bass_kernel_spmd as _run

    a = {n.removeprefix("L0_conv_"): _np.asarray(v) for n, v in inputs.items()}

    def on_partitions(v):
        return v.reshape(CHUNKS, P, -1).transpose(1, 0, 2)

    names = [f"{b}_{f}" for f in ("gamma", "beta", "mean", "var") for b in ("edge", "bn1", "bn2")]
    columns = [a[n].reshape(CHANNELS, 1) for n in names + ["fusion_b", "balance_b"]]
    columns += [a[n].reshape(CHANNELS, 9) for n in ("edge_w", "deform_w")]
    laid = {
        "x": a["x"],
        "params": on_partitions(_np.concatenate(columns, axis=1)).transpose(0, 2, 1).reshape(P, -1),
        "w1_t": a["fusion_w"].T.reshape(2 * CHUNKS, P, CHANNELS).transpose(1, 0, 2),
        "w2_t": on_partitions(a["balance_w"].T),
        "fc1_t": on_partitions(a["fc1_w"].T),
        "fc2_t": a["fc2_w"].T,
    }
    nc = _bacc.Bacc("TRN2", target_bir_lowering=False, num_devices=1)
    arrays, args = {}, []
    for name, v in laid.items():
        v = _np.ascontiguousarray(v)
        arrays[f"in_{name}"] = v
        args.append(nc.dram_tensor(f"in_{name}", v.shape, _mybir.dt.from_np(v.dtype), kind="ExternalInput").ap())
    shape = (IMAGES, CHANNELS, HEIGHT, WIDTH)
    args.append(nc.dram_tensor("out_0", shape, _mybir.dt.float32, kind="ExternalOutput").ap())
    build(nc, *args)
    return _run(nc, [arrays], core_ids=[0]).results[0]["out_0"]
```

```python
import concourse.bass as bass
from concourse import mybir
from contextlib import ExitStack

IMAGES, CHANNELS, HEIGHT, WIDTH = 32, 256, 64, 64
P = 128
CHUNKS = CHANNELS // P
ROWS = 16
STRIPS = HEIGHT // ROWS
TOTAL = IMAGES * STRIPS
SIZE = ROWS * WIDTH
HALF = SIZE // 2
HALF_ROWS = ROWS // 2
RING = 2 * STRIPS
PAIRS = IMAGES // 2
PITCH = WIDTH + 1
HIDDEN = CHANNELS // 16
EPS = 1e-5

GAMMA, BETA, MEAN, VAR, BIAS, TAPS = 0, 6, 12, 18, 24, 28
PARAMS = TAPS + 2 * 9 * CHUNKS

PE_TAPS = [[(0, 0), (0, -1), (0, 1), (1, -1), (1, 1)], [(0, 0), (0, -1), (0, 1), (1, -1)]]
DVE_TAPS = [[(-1, 0), (1, 0), (-1, -1), (-1, 1)], [(-1, 0), (1, 0), (-1, -1), (-1, 1), (1, 1)]]
CENTRE = (0, 0)
TURNS = [(1, 1, 2, 2, 1, 2, 2, 1, 2, 2, 2), (1, 1, 2, 1, 2, 2, 1, 2, 2, 1, 2, 2)]
SIDE = (1, 1)
MIX_TAPS = [(dy, dx) for dy in (-1, 0, 1) for dx in (-1, 0, 1) if (dy, dx) not in (CENTRE, SIDE)]


def build(nc: bass.Bass, x, params, w1_t, w2_t, fc1_t, fc2_t, out):
    f32, f32r = mybir.dt.float32, mybir.dt.float32r
    ACT, ALU = mybir.ActivationFunctionType, mybir.AluOpType

    with ExitStack() as ctx:
        def sb(name, shape, dt=f32):
            return ctx.enter_context(nc.sbuf_tensor(name, shape, dt))

        def sem(name):
            return ctx.enter_context(nc.semaphore(name))

        xring = sb("xring", [P, 2, CHUNKS, HEIGHT * WIDTH])
        split_size = (ROWS + 1) * PITCH + 3
        xhi = sb("xhi", [P, 2, CHUNKS, split_size], f32r)
        xlo = sb("xlo", [P, 2, CHUNKS, split_size], f32r)
        mix_size = (HEIGHT + 2) * PITCH + 2
        mix = sb("mix", [P, CHUNKS, mix_size])
        edge = sb("edge", [P, CHUNKS, SIZE])
        ehi = sb("ehi", [P, CHUNKS, SIZE], f32r)
        elo = sb("elo", [P, CHUNKS, SIZE], f32r)
        y = sb("y", [P, CHUNKS, SIZE])
        yhi = sb("yhi", [P, CHUNKS, SIZE], f32r)
        ylo = sb("ylo", [P, CHUNKS, SIZE], f32r)
        side = sb("side", [P, SIZE])
        w1x_att = sb("w1x_att", [P, CHUNKS, CHANNELS])
        unused = w1x_att[:].rearrange("p k o -> p (k o)").bitcast(mybir.dt.bfloat16)
        gain = sb("gain", [P, CHUNKS, SIZE])
        w1x = sb("w1x", [P, CHUNKS, CHANNELS])
        w1x_hi = sb("w1x_hi", [P, CHUNKS, CHANNELS], f32r)
        w1x_lo = sb("w1x_lo", [P, CHUNKS, CHANNELS], f32r)
        w1e_hi = sb("w1e_hi", [P, CHUNKS, CHANNELS], f32r)
        w1e_lo = sb("w1e_lo", [P, CHUNKS, CHANNELS], f32r)
        w2_hi = sb("w2_hi", [P, CHUNKS, CHANNELS], f32r)
        w2_lo = sb("w2_lo", [P, CHUNKS, CHANNELS], f32r)
        diag_hi = sb("diag_hi", [P, sum(map(len, PE_TAPS)), P], f32r)
        diag_lo = sb("diag_lo", [P, sum(map(len, PE_TAPS)), P], f32r)
        prm = sb("prm", [P, PARAMS])
        tap_hi = sb("tap_hi", [P, 9 * CHUNKS], f32r)
        tap_lo = sb("tap_lo", [P, 9 * CHUNKS])
        bn = sb("bn", [P, 4, 6])
        fc1 = sb("fc1", [P, CHUNKS, HIDDEN])
        fc2 = sb("fc2", [HIDDEN, CHANNELS])
        sums = sb("sums", [P, 2, CHUNKS, STRIPS])
        hidden = sb("hidden", [HIDDEN, 1])
        att = sb("att", [P, CHUNKS])
        w1e_raw = gain[:, 0, 0:2 * CHANNELS].rearrange("p (k o) -> p k o", k=CHUNKS)
        w2_raw = gain[:, 0, 2 * CHANNELS:4 * CHANNELS].rearrange("p (k o) -> p k o", k=CHUNKS)
        ident = gain[:, 1, 0:P]

        acc1 = ctx.enter_context(nc.psum_tensor("acc1", [P, CHUNKS, SIZE], f32))
        acc2 = ctx.enter_context(nc.psum_tensor("acc2", [P, SIZE], f32))
        prod = ctx.enter_context(nc.psum_tensor("prod", [P, 2, HALF], f32))

        x_loaded = [sem(f"x_loaded{i}") for i in range(RING)]
        x_stored = [sem(f"x_stored{i}") for i in range(RING)]
        params_loaded, weights_loaded = sem("params_loaded"), sem("weights_loaded")
        pads_zeroed, ident_ready = sem("pads_zeroed"), sem("ident_ready")
        setup_step, root_ready = sem("setup_step"), sem("root_ready")
        his_ready, weights_ready = sem("his_ready"), sem("weights_ready")
        x_summed = sem("x_summed")
        xhi_ready, xlo_ready = sem("xhi_ready"), sem("xlo_ready")
        taps_on_pe = sem("taps_on_pe")
        acc1_tap = [sem(f"acc1_tap{c}") for c in range(CHUNKS)]
        edge_ready = sem("edge_ready")
        ehi_ready, elo_ready = sem("ehi_ready"), sem("elo_ready")
        w1_done, w2_done = sem("w1_done"), sem("w2_done")
        mix_ready = [sem(f"mix_ready{c}") for c in range(CHUNKS)]
        acc2_begun = sem("acc2_begun")
        acc2_tap = [sem(f"acc2_tap{c}") for c in range(CHUNKS)]
        side_ready, y_summed = sem("side_ready"), sem("y_summed")
        yhi_ready, ylo_ready = sem("yhi_ready"), sem("ylo_ready")
        gain_ready = [sem(f"gain_ready{c}") for c in range(CHUNKS)]
        out_ready = sem("out_ready")
        fc1_done, hidden_ready = sem("fc1_done"), sem("hidden_ready")
        fc2_done, att_ready = sem("fc2_done"), sem("att_ready")
        w1x_att_ready = sem("w1x_att_ready")
        w1x_hi_ready, w1x_lo_ready = sem("w1x_hi_ready"), sem("w1x_lo_ready")

        block = ctx.enter_context(nc.Block())

        def exists(pair, k):
            return not isinstance(pair, int) or 0 <= pair * RING + k < TOTAL

        def count(per_strip, pair, k, extra=0):
            return pair * (RING * per_strip) + (k * per_strip + extra)

        def image_count(per_image, pair, k, extra):
            return pair * (2 * per_image) + (k // STRIPS * per_image + extra)

        def min_count(per_strip, pair, k):
            return count(per_strip, pair, k) if exists(pair, k - 1) else per_strip * TOTAL

        def turns(pair, k):
            return pair * 16 + 16 * (k // RING + 1)

        def first(k):
            return k % STRIPS == 0

        def last(k):
            return k % STRIPS == STRIPS - 1

        def tap_of(conv, tap, c):
            dy, dx = tap
            return TAPS + (conv * 9 + (dy + 1) * 3 + dx + 1) * CHUNKS + c

        def x_rows(k, c, row, rows, col=0, cols=WIDTH):
            at = (k % STRIPS) * ROWS + row
            image = xring[:, (k // STRIPS) % 2, c, at * WIDTH:(at + rows) * WIDTH]
            return image.rearrange("p (r w) -> p r w", w=WIDTH)[:, :, col:col + cols]

        def padded(row_tile, row, rows, dx=0):
            at = row * PITCH + 1 + dx
            return row_tile[:, at:at + rows * PITCH].rearrange("p (r w) -> p r w", w=PITCH)[:, :, 0:WIDTH]

        def written(row_tile, row, rows):
            return padded(row_tile, row, rows)

        def steps(eng, step):
            for k in range(-4, 4):
                step(0, k)
            with eng.Fori(0, PAIRS - 1) as pair:
                for k in range(4, 4 + RING):
                    step(pair, k)
            for k in range(4, 4 + RING):
                step(PAIRS - 1, k)

        x_pairs, out_pairs = (t.rearrange("(n i) (k p) h w -> n i p k (h w)", i=2, p=P) for t in (x, out))

        def load(sp, pair, slot):
            i, at = slot // STRIPS, (slot % STRIPS) * SIZE
            sp.dma_start(xring[:, i, :, at:at + SIZE], x_pairs[pair, i, :, :, at:at + SIZE]
                         ).then_inc(x_loaded[slot], 16)

        def store(sp, pair, slot):
            sp.wait_ge(out_ready, pair * (2 * RING) + (2 * slot + 2))
            i, at = slot // STRIPS, (slot % STRIPS) * SIZE
            sp.dma_start(out_pairs[pair, i, :, :, at:at + SIZE], xring[:, i, :, at:at + SIZE]
                         ).then_inc(x_stored[slot], 16)

        @block.sync
        def _(sp):
            load(sp, 0, 0)
            sp.dma_start(prm[:], params).then_inc(params_loaded, 16)
            sp.dma_start(w1x[:], w1_t[:, 0:CHUNKS, :]).then_inc(weights_loaded, 16)
            sp.dma_start(w1e_raw, w1_t[:, CHUNKS:2 * CHUNKS, :]).then_inc(weights_loaded, 16)
            sp.dma_start(w2_raw, w2_t).then_inc(weights_loaded, 16)
            sp.dma_start(fc1[:], fc1_t).then_inc(weights_loaded, 16)
            sp.dma_start(fc2[:], fc2_t).then_inc(weights_loaded, 16)
            for slot in range(1, RING):
                load(sp, 0, slot)
            with sp.Fori(0, PAIRS - 1) as pair:
                for slot in range(RING):
                    store(sp, pair, slot)
                    sp.wait_ge(x_stored[slot], pair * 16 + 16)
                    load(sp, pair + 1, slot)
            for slot in range(RING):
                store(sp, PAIRS - 1, slot)
            for slot in range(RING):
                sp.wait_ge(x_stored[slot], 16 * (PAIRS))

        @block.tensor
        def _(pe):
            pe.wait_ge(pads_zeroed, 1)
            pe.wait_ge(weights_ready, 1)

            def conv_taps(pair, k, c, half):
                buf = k % 2
                jobs = [(w, v) for w, v in ((diag_hi, xhi), (diag_lo, xhi), (diag_hi, xlo))]
                for job, (w, v) in enumerate(jobs):
                    if half == 0 and job == 0:
                        pe.wait_ge(xhi_ready, count(2, pair, k, c + 1))
                    if half == 0 and job == 2:
                        pe.wait_ge(xlo_ready, count(2, pair, k, c + 1))
                    for t, (dy, dx) in enumerate(PE_TAPS[c]):
                        rows = HALF_ROWS - (last(k) and half == 1 and dy == 1)
                        at = half * HALF
                        mm = nc.tensor.matmul(
                            acc1[:, c, at:at + rows * WIDTH], w[:, c * len(PE_TAPS[0]) + t, :],
                            padded(v[:, buf, c, :], half * HALF_ROWS + dy, rows, dx),
                            start=(job == 0 and t == 0), stop=(job == 2 and t == len(PE_TAPS[c]) - 1))
                return mm

            def step(pair, k):
                conv, image = exists(pair, k + 1), exists(pair, k) and first(k)
                if conv:
                    if exists(pair, k):
                        pe.wait_ge(edge_ready, count(2, pair, k, 1))
                    conv_taps(pair, k + 1, 0, 0)
                if image:
                    pe.wait_ge(x_summed, count(2, pair, k, 2 * STRIPS))
                    if exists(pair, k - 4):
                        pe.wait_ge(gain_ready[1], count(2, pair, k - 4, 1))
                    for n in range(CHUNKS * STRIPS):
                        c, s = n // STRIPS, n % STRIPS
                        mm = nc.tensor.matmul(prod[0:HIDDEN, 0, 0:1], fc1[:, c, :],
                                              sums[:, (k // STRIPS) % 2, c, s:s + 1],
                                              start=(n == 0), stop=(n == CHUNKS * STRIPS - 1))
                    mm.then_inc(fc1_done, 1)
                if conv:
                    conv_taps(pair, k + 1, 0, 1).then_inc(taps_on_pe, 1)
                if image:
                    pe.wait_ge(hidden_ready, image_count(1, pair, k, 1))
                    if exists(pair, k - 4):
                        pe.wait_ge(gain_ready[1], count(2, pair, k - 4, 2))
                    for c in range(CHUNKS):
                        mm = nc.tensor.matmul(prod[:, 1, c:c + 1], fc2[:, c * P:(c + 1) * P],
                                              hidden[:], start=True, stop=True)
                    mm.then_inc(fc2_done, 1)
                if conv:
                    if exists(pair, k):
                        pe.wait_ge(edge_ready, count(2, pair, k, 2))
                    conv_taps(pair, k + 1, 1, 0)
                    conv_taps(pair, k + 1, 1, 1).then_inc(taps_on_pe, 1)

                if exists(pair, k):
                    buf = k % 2
                    for u in range(4):
                        o, half = u // 2, u % 2
                        if u == 0:
                            pe.wait_ge(w1x_hi_ready, image_count(1, pair, k, 1))
                            if exists(pair, k - 4):
                                pe.wait_ge(gain_ready[1], count(2, pair, k - 4, 1))
                        elif u == 1:
                            if exists(pair, k - 4):
                                pe.wait_ge(gain_ready[1], count(2, pair, k - 4, 2))
                        else:
                            pe.wait_ge(mix_ready[0], count(2, pair, k, u - 1))
                        jobs = []
                        for cc in range(CHUNKS):
                            v, l = (padded(b[:, buf, cc, :], half * HALF_ROWS, HALF_ROWS) for b in (xhi, xlo))
                            jobs += [(w1x_hi, cc, v, None), (w1x_hi, cc, l, None), (w1x_lo, cc, v, "att")]
                        for cc in range(CHUNKS):
                            v, l = (b[:, cc, half * HALF:(half + 1) * HALF] for b in (ehi, elo))
                            jobs += [(w1e_hi, cc, v, "ehi"), (w1e_lo, cc, v, None), (w1e_hi, cc, l, "elo")]
                        for n, (w, cc, v, needs) in enumerate(jobs):
                            if u == 0 and needs == "att":
                                pe.wait_ge(w1x_lo_ready, image_count(1, pair, k, 1))
                            if u == 0 and needs == "ehi":
                                pe.wait_ge(ehi_ready, count(2, pair, k, cc + 1))
                            if u == 0 and needs == "elo":
                                pe.wait_ge(elo_ready, count(2, pair, k, cc + 1))
                            mm = nc.tensor.matmul(prod[:, u % 2, :], w[:, cc, o * P:(o + 1) * P], v,
                                                  start=(n == 0), stop=(n == len(jobs) - 1))
                        mm.then_inc(w1_done, 1)

                if exists(pair, k - 3):
                    for u in range(4):
                        o, half = u // 2, u % 2
                        if u < 2:
                            if exists(pair, k):
                                pe.wait_ge(mix_ready[1], count(2, pair, k, u + 1))
                            else:
                                pe.wait_ge(gain_ready[1], count(2, pair, k - 4, u + 1))
                        else:
                            pe.wait_ge(gain_ready[0], count(2, pair, k - 3, u - 1))
                        jobs = []
                        for cc in range(CHUNKS):
                            v, l = (b[:, cc, half * HALF:(half + 1) * HALF] for b in (yhi, ylo))
                            jobs += [(w2_hi, cc, v, "yhi"), (w2_lo, cc, v, None), (w2_hi, cc, l, "ylo")]
                        for n, (w, cc, v, needs) in enumerate(jobs):
                            if u == 0 and needs == "yhi":
                                pe.wait_ge(yhi_ready, count(2, pair, k - 3, cc + 1))
                            if u == 0 and needs == "ylo":
                                pe.wait_ge(ylo_ready, count(2, pair, k - 3, cc + 1))
                            mm = nc.tensor.matmul(prod[:, u % 2, :], w[:, cc, o * P:(o + 1) * P], v,
                                                  start=(n == 0), stop=(n == len(jobs) - 1))
                        mm.then_inc(w2_done, 1)

            steps(pe, step)

        @block.scalar
        def _(act):
            act.wait_ge(setup_step, 1)
            nc.scalar.activation(bn[:, 3, :], bn[:, 2, :], ACT.Sqrt).then_inc(root_ready, 1)
            act.wait_ge(weights_loaded, 5 * 16)
            nc.scalar.activation(w1e_hi[:], w1e_raw, ACT.Copy).then_inc(his_ready, 1)
            nc.scalar.activation(w2_hi[:], w2_raw, ACT.Copy).then_inc(his_ready, 1)
            act.wait_ge(params_loaded, 16)
            nc.scalar.activation(tap_hi[:], prm[:, TAPS:TAPS + 9 * CHUNKS], ACT.Copy).then_inc(his_ready, 1)
            act.wait_ge(pads_zeroed, 1)

            def sum_x(pair, k):
                act.wait_ge(x_loaded[k % RING], turns(pair, k))
                if exists(pair, k - 4):
                    act.wait_ge(w1x_lo_ready, image_count(1, pair, k - 4, 1))
                for c in range(CHUNKS):
                    if exists(pair, k - 1) or c:
                        act.wait_ge(x_summed, count(2, pair, k, c))
                    nc.scalar.activation(unused.rearrange("p (r w) -> p r w", w=WIDTH),
                                         x_rows(k, c, 0, ROWS), ACT.Copy,
                                         accum_out=sums[:, (k // STRIPS) % 2, c, k % STRIPS:k % STRIPS + 1]
                                         ).then_inc(x_summed, 1)

            def round_x(pair, k, c):
                if c == 0:
                    act.wait_ge(x_loaded[k % RING], turns(pair, k))
                    if not last(k):
                        act.wait_ge(x_loaded[(k + 1) % RING], turns(pair, k + 1))
                    if exists(pair, k - 2):
                        act.wait_ge(w1_done, count(4, pair, k - 2, 4))
                rows = ROWS + (not last(k))
                nc.scalar.activation(written(xhi[:, k % 2, c, :], 0, rows), x_rows(k, c, 0, rows),
                                     ACT.Copy).then_inc(xhi_ready, 1)

            def edge_out(pair, k, c):
                act.wait_ge(acc1_tap[c], count(len(DVE_TAPS[c]), pair, k + 1))
                if exists(pair, k - 1):
                    act.wait_ge(ehi_ready, count(2, pair, k - 1, c + 1))
                    act.wait_ge(elo_ready, count(2, pair, k - 1, c + 1))
                if isinstance(pair, int) and pair == 0 and k == 0 and c == 0:
                    act.wait_ge(weights_ready, 1)
                nc.scalar.activation(edge[:, c, :], acc1[:, c, :], ACT.Relu, bias=bn[:, 1, c:c + 1],
                                     scale=bn[:, 0, c:c + 1]).then_inc(edge_ready, 1)

            def round_edge(pair, k, c):
                act.wait_ge(edge_ready, count(2, pair, k, c + 1))
                if exists(pair, k - 1):
                    act.wait_ge(w1_done, count(4, pair, k))
                nc.scalar.activation(ehi[:, c, :], edge[:, c, :], ACT.Copy).then_inc(ehi_ready, 1)

            def mix_out(pair, k, u):
                o, half = u // 2, u % 2
                act.wait_ge(w1_done, count(4, pair, k, u + 1))
                if exists(pair, k - 3):
                    act.wait_ge(acc2_tap[o], count(len(MIX_TAPS), pair, k - 2))
                rows = written(mix[:, o, :], 1 + (k % STRIPS) * ROWS + half * HALF_ROWS, HALF_ROWS)
                nc.scalar.activation(rows, prod[:, u % 2, :].rearrange("p (r w) -> p r w", w=WIDTH),
                                     ACT.Identity, bias=bn[:, 1, 2 + o:3 + o],
                                     scale=bn[:, 0, 2 + o:3 + o]).then_inc(mix_ready[o], 1)

            def begin_acc2(pair, k, c):
                act.wait_ge(mix_ready[c], count(2, pair, k, 2))
                if c:
                    act.wait_ge(acc2_tap[0], count(len(MIX_TAPS), pair, k + 1))
                elif exists(pair, k - 1):
                    act.wait_ge(acc2_tap[1], count(len(MIX_TAPS), pair, k))
                at = tap_of(1, CENTRE, c)
                nc.scalar.activation(acc2[:].rearrange("p (r w) -> p r w", w=WIDTH),
                                     padded(mix[:, c, :], 1 + (k % STRIPS) * ROWS, ROWS),
                                     ACT.Copy, scale=prm[:, at:at + 1]).then_inc(acc2_begun, 1)

            def side_out(pair, k, c):
                if last(k):
                    act.wait_ge(mix_ready[c], count(2, pair, k, 2))
                else:
                    act.wait_ge(mix_ready[c], count(2, pair, k + 1, 1))
                if exists(pair, k - 1) or c:
                    act.wait_ge(y_summed, count(2, pair, k, c))
                at = tap_of(1, SIDE, c)
                nc.scalar.activation(side[:].rearrange("p (r w) -> p r w", w=WIDTH),
                                     padded(mix[:, c, :], 1 + (k % STRIPS) * ROWS + SIDE[0], ROWS, SIDE[1]),
                                     ACT.Copy, scale=prm[:, at:at + 1]).then_inc(side_ready, 1)

            def round_y(pair, k, c):
                act.wait_ge(y_summed, count(2, pair, k, c + 1))
                if exists(pair, k - 1):
                    act.wait_ge(w2_done, count(4, pair, k))
                nc.scalar.activation(yhi[:, c, :], y[:, c, :], ACT.Copy).then_inc(yhi_ready, 1)

            def gain_out(pair, k, u):
                o, half = u // 2, u % 2
                act.wait_ge(w2_done, count(4, pair, k, u + 1))
                if exists(pair, k - 1):
                    act.wait_ge(out_ready, count(2, pair, k - 1, o + 1))
                nc.scalar.activation(gain[:, o, half * HALF:(half + 1) * HALF], prod[:, u % 2, :],
                                     ACT.Identity, bias=bn[:, 1, 4 + o:5 + o],
                                     scale=bn[:, 0, 4 + o:5 + o]).then_inc(gain_ready[o], 1)

            def hide(pair, k):
                act.wait_ge(fc1_done, image_count(1, pair, k, 1))
                nc.scalar.activation(hidden[:], prod[0:HIDDEN, 0, 0:1], ACT.Relu,
                                     scale=1.0 / (HEIGHT * WIDTH)).then_inc(hidden_ready, 1)

            def attend(pair, k):
                act.wait_ge(fc2_done, image_count(1, pair, k, 1))
                nc.scalar.activation(att[:], prod[:, 1, 0:CHUNKS], ACT.Sigmoid).then_inc(att_ready, 1)
                act.wait_ge(att_ready, image_count(1, pair, k, 1))
                act.wait_ge(x_summed, min_count(2, pair, k + 4))
                for c in range(CHUNKS):
                    nc.scalar.activation(w1x_att[:, c, :], w1x[:, c, :], ACT.Copy,
                                         scale=att[:, c:c + 1]).then_inc(w1x_att_ready, 1)
                if exists(pair, k - 1):
                    act.wait_ge(w1_done, count(4, pair, k))
                act.wait_ge(w1x_att_ready, image_count(2, pair, k, 2))
                nc.scalar.activation(w1x_hi[:], w1x_att[:], ACT.Copy).then_inc(w1x_hi_ready, 1)

            def step(pair, k):
                now, y_next, gain_now = exists(pair, k), exists(pair, k - 2), exists(pair, k - 3)
                if gain_now:
                    round_y(pair, k - 3, 0)
                if now and first(k):
                    hide(pair, k)
                if now:
                    edge_out(pair, k, 1)
                if y_next:
                    begin_acc2(pair, k - 2, 0)
                if now:
                    round_edge(pair, k, 1)
                    if first(k):
                        attend(pair, k)
                if gain_now:
                    round_y(pair, k - 3, 1)
                if y_next:
                    side_out(pair, k - 2, 0)
                if now:
                    mix_out(pair, k, 0)
                    mix_out(pair, k, 1)
                if y_next:
                    begin_acc2(pair, k - 2, 1)
                if now:
                    mix_out(pair, k, 2)
                if exists(pair, k + 1):
                    edge_out(pair, k + 1, 0)
                if now:
                    mix_out(pair, k, 3)
                if gain_now:
                    gain_out(pair, k - 3, 0)
                if exists(pair, k + 2):
                    round_x(pair, k + 2, 0)
                if gain_now:
                    gain_out(pair, k - 3, 1)
                if exists(pair, k + 2):
                    round_x(pair, k + 2, 1)
                if exists(pair, k + 1):
                    round_edge(pair, k + 1, 0)
                if gain_now:
                    gain_out(pair, k - 3, 2)
                    gain_out(pair, k - 3, 3)
                if exists(pair, k + 4):
                    sum_x(pair, k + 4)
                if y_next:
                    side_out(pair, k - 2, 1)

            steps(act, step)

        @block.vector
        def _(dve):
            made = [0]

            def link(ins):
                made[0] += 1
                ins.then_inc(setup_step, 1)
                dve.wait_ge(setup_step, made[0])

            scale, shift, v, r = (bn[:, n, :] for n in range(4))
            t = y[:, 0, 0:6]
            dve.wait_ge(params_loaded, 16)
            link(nc.vector.tensor_scalar(v, prm[:, VAR:VAR + 6], EPS, None, ALU.add))
            link(nc.vector.tensor_tensor(prm[:, MEAN + 2:MEAN + 6], prm[:, MEAN + 2:MEAN + 6],
                                         prm[:, BIAS:BIAS + 4], ALU.subtract))
            dve.wait_ge(root_ready, 1)
            link(nc.vector.reciprocal(r, r))
            link(nc.vector.tensor_tensor(t, r, r, ALU.mult))
            link(nc.vector.tensor_tensor(t, t, v, ALU.mult))
            link(nc.vector.tensor_scalar(t, t, -0.5, 1.5, ALU.mult, ALU.add))
            link(nc.vector.tensor_tensor(r, r, t, ALU.mult))
            link(nc.vector.tensor_tensor(scale, r, prm[:, GAMMA:GAMMA + 6], ALU.mult))
            link(nc.vector.tensor_tensor(t, scale, prm[:, MEAN:MEAN + 6], ALU.mult))
            link(nc.vector.tensor_tensor(shift, prm[:, BETA:BETA + 6], t, ALU.subtract))
            dve.wait_ge(his_ready, 3)
            nc.vector.tensor_tensor(w1e_lo[:], w1e_raw, w1e_hi[:].bitcast(f32), ALU.subtract)
            nc.vector.tensor_tensor(w2_lo[:], w2_raw, w2_hi[:].bitcast(f32), ALU.subtract)
            link(nc.vector.tensor_tensor(tap_lo[:], prm[:, TAPS:TAPS + 9 * CHUNKS], tap_hi[:].bitcast(f32),
                                         ALU.subtract))
            dve.wait_ge(ident_ready, 2)
            for n, (c, tap) in enumerate((c, tap) for c in range(CHUNKS) for tap in PE_TAPS[c]):
                at = tap_of(0, tap, c) - TAPS
                nc.vector.tensor_scalar(diag_hi[:, n, :], ident, tap_hi[:, at:at + 1].bitcast(f32),
                                        None, ALU.mult)
                made_last = nc.vector.tensor_scalar(diag_lo[:, n, :], ident, tap_lo[:, at:at + 1],
                                                    None, ALU.mult)
            made_last.then_inc(weights_ready, 1)

            def acc1_op(pair, k, c, n):
                if n == 0:
                    dve.wait_ge(taps_on_pe, count(2, pair, k, c + 1))
                else:
                    dve.wait_ge(acc1_tap[c], count(len(DVE_TAPS[c]), pair, k, n))
                dy, dx = DVE_TAPS[c][n]
                top = 1 if first(k) and dy < 0 else 0
                rows = ROWS - top - (1 if last(k) and dy > 0 else 0)
                col, cols = max(0, -dx), WIDTH - abs(dx)
                acc = acc1[:, c, top * WIDTH:(top + rows) * WIDTH].rearrange("p (r w) -> p r w", w=WIDTH)
                acc = acc[:, :, col:col + cols]
                at = tap_of(0, (dy, dx), c)
                nc.vector.scalar_tensor_tensor(
                    out=acc, in0=x_rows(k, c, top + dy, rows, col + dx, cols), scalar=prm[:, at:at + 1],
                    in1=acc, op0=ALU.mult, op1=ALU.add).then_inc(acc1_tap[c], 1)

            def acc2_op(pair, k, c, n):
                if n == 0:
                    dve.wait_ge(acc2_begun, count(2, pair, k, c + 1))
                    if not last(k):
                        dve.wait_ge(mix_ready[c], count(2, pair, k + 1, 1))
                else:
                    dve.wait_ge(acc2_tap[c], count(len(MIX_TAPS), pair, k, n))
                final = n == len(MIX_TAPS) - 1
                if final and exists(pair, k - 1):
                    dve.wait_ge(yhi_ready, count(2, pair, k - 1, c + 1))
                    dve.wait_ge(ylo_ready, count(2, pair, k - 1, c + 1))
                acc = acc2[:].rearrange("p (r w) -> p r w", w=WIDTH)
                to = y[:, c, :].rearrange("p (r w) -> p r w", w=WIDTH) if final else acc
                dy, dx = MIX_TAPS[n]
                at = tap_of(1, (dy, dx), c)
                nc.vector.scalar_tensor_tensor(
                    out=to, in0=padded(mix[:, c, :], 1 + (k % STRIPS) * ROWS + dy, ROWS, dx),
                    scalar=prm[:, at:at + 1], in1=acc, op0=ALU.mult, op1=ALU.add).then_inc(acc2_tap[c], 1)

            def step(pair, k):
                for c in range(CHUNKS):
                    taps = {1: 0, 2: 0}
                    for conv in TURNS[c]:
                        if conv == 1 and exists(pair, k + 1):
                            acc1_op(pair, k + 1, c, taps[1])
                        if conv == 2 and exists(pair, k - 2):
                            acc2_op(pair, k - 2, c, taps[2])
                        taps[conv] += 1

            steps(dve, step)

        @block.gpsimd
        def _(pool):
            pool.memset(ident, 0.0).then_inc(ident_ready, 1)
            pool.wait_ge(ident_ready, 1)
            pool.affine_select(out=ident, in_=ident, compare_op=ALU.not_equal, fill=1.0, base=0,
                               pattern=[[-1, P]], channel_multiplier=1).then_inc(ident_ready, 1)
            for c in range(CHUNKS):
                for buf in range(2):
                    for tile in (xhi, xlo):
                        pool.memset(tile[:, buf, c, 0:(ROWS + 1) * PITCH + 1:PITCH].bitcast(f32), 0.0)
                pool.memset(mix[:, c, 0:PITCH + 1], 0.0)
                pool.memset(mix[:, c, 2 * PITCH:(HEIGHT + 1) * PITCH:PITCH], 0.0)
                zeroed = pool.memset(mix[:, c, (HEIGHT + 1) * PITCH:mix_size], 0.0)
            zeroed.then_inc(pads_zeroed, 1)

            def rest_of_x(pair, k, c):
                pool.wait_ge(xhi_ready, count(2, pair, k, c + 1))
                rows = ROWS + (not last(k))
                nc.gpsimd.tensor_tensor(written(xlo[:, k % 2, c, :], 0, rows), x_rows(k, c, 0, rows),
                                        written(xhi[:, k % 2, c, :], 0, rows).bitcast(f32), ALU.subtract
                                        ).then_inc(xlo_ready, 1)

            def rest_of_edge(pair, k, c):
                pool.wait_ge(ehi_ready, count(2, pair, k, c + 1))
                nc.gpsimd.tensor_tensor(elo[:, c, :], edge[:, c, :], ehi[:, c, :].bitcast(f32), ALU.subtract
                                        ).then_inc(elo_ready, 1)

            def rest_of_y(pair, k, c):
                pool.wait_ge(yhi_ready, count(2, pair, k, c + 1))
                nc.gpsimd.tensor_tensor(ylo[:, c, :], y[:, c, :], yhi[:, c, :].bitcast(f32), ALU.subtract
                                        ).then_inc(ylo_ready, 1)

            def add_side(pair, k, c):
                pool.wait_ge(acc2_tap[c], count(len(MIX_TAPS), pair, k + 1))
                pool.wait_ge(side_ready, count(2, pair, k, c + 1))
                nc.gpsimd.tensor_tensor(y[:, c, :], y[:, c, :], side[:], ALU.add).then_inc(y_summed, 1)

            def rest_of_w1x(pair, k):
                pool.wait_ge(w1x_hi_ready, image_count(1, pair, k, 1))
                nc.gpsimd.tensor_tensor(w1x_lo[:], w1x_att[:], w1x_hi[:].bitcast(f32), ALU.subtract
                                        ).then_inc(w1x_lo_ready, 1)

            def times_x(pair, k, c):
                pool.wait_ge(gain_ready[c], count(2, pair, k, 2))
                at = (k % STRIPS) * SIZE
                strip = xring[:, (k // STRIPS) % 2, c, at:at + SIZE]
                nc.gpsimd.tensor_tensor(strip, strip, gain[:, c, :], ALU.mult).then_inc(out_ready, 1)

            def step(pair, k):
                if exists(pair, k):
                    rest_of_edge(pair, k, 1)
                if exists(pair, k - 3):
                    add_side(pair, k - 3, 1)
                if exists(pair, k) and first(k):
                    rest_of_w1x(pair, k)
                if exists(pair, k - 3):
                    rest_of_y(pair, k - 3, 0)
                    rest_of_y(pair, k - 3, 1)
                if exists(pair, k - 2):
                    add_side(pair, k - 2, 0)
                if exists(pair, k + 2):
                    rest_of_x(pair, k + 2, 0)
                    rest_of_x(pair, k + 2, 1)
                if exists(pair, k + 1):
                    rest_of_edge(pair, k + 1, 0)
                if exists(pair, k - 3):
                    times_x(pair, k - 3, 0)
                    times_x(pair, k - 3, 1)

            steps(pool, step)


def kernel(**inputs):
    import numpy as _np
    import concourse.bacc as _bacc
    from concourse import mybir as _mybir
    from concourse.bass_utils import run_bass_kernel_spmd as _run

    a = {n.removeprefix("L0_conv_"): _np.asarray(v) for n, v in inputs.items()}

    def on_partitions(v):
        return v.reshape(CHUNKS, P, -1).transpose(1, 0, 2)

    names = [f"{b}_{f}" for f in ("gamma", "beta", "mean", "var") for b in ("edge", "bn1", "bn2")]
    columns = [a[n].reshape(CHANNELS, 1) for n in names + ["fusion_b", "balance_b"]]
    columns += [a[n].reshape(CHANNELS, 9) for n in ("edge_w", "deform_w")]
    laid = {
        "x": a["x"],
        "params": on_partitions(_np.concatenate(columns, axis=1)).transpose(0, 2, 1).reshape(P, -1),
        "w1_t": a["fusion_w"].T.reshape(2 * CHUNKS, P, CHANNELS).transpose(1, 0, 2),
        "w2_t": on_partitions(a["balance_w"].T),
        "fc1_t": on_partitions(a["fc1_w"].T),
        "fc2_t": a["fc2_w"].T,
    }
    nc = _bacc.Bacc("TRN2", target_bir_lowering=False, num_devices=1,
                    dynamic_dma_scratch_size=1024)
    arrays, args = {}, []
    for name, v in laid.items():
        v = _np.ascontiguousarray(v)
        arrays[f"in_{name}"] = v
        args.append(nc.dram_tensor(f"in_{name}", v.shape, _mybir.dt.from_np(v.dtype), kind="ExternalInput").ap())
    shape = (IMAGES, CHANNELS, HEIGHT, WIDTH)
    args.append(nc.dram_tensor("out_0", shape, _mybir.dt.float32, kind="ExternalOutput").ap())
    build(nc, *args)
    return _run(nc, [arrays], core_ids=[0]).results[0]["out_0"]
```

```python
import concourse.bass as bass
from concourse import mybir
from contextlib import ExitStack

IMAGES, CHANNELS, HEIGHT, WIDTH = 32, 256, 64, 64
P = 128
CHUNKS = CHANNELS // P
ROWS = 16
STRIPS = HEIGHT // ROWS
TOTAL = IMAGES * STRIPS
SIZE = ROWS * WIDTH
HALF = SIZE // 2
HALF_ROWS = ROWS // 2
RING = 2 * STRIPS
PAIRS = IMAGES // 2
PITCH = WIDTH + 1
HIDDEN = CHANNELS // 16
EPS = 1e-5

GAMMA, BETA, MEAN, VAR, BIAS, TAPS = 0, 6, 12, 18, 24, 28
PARAMS = TAPS + 2 * 9 * CHUNKS

PE_TAPS = [[(0, 0), (0, -1), (0, 1), (1, -1), (1, 1)], [(0, 0), (0, -1), (0, 1), (1, -1)]]
DVE_TAPS = [[(-1, 0), (1, 0), (-1, -1), (-1, 1)], [(-1, 0), (1, 0), (-1, -1), (-1, 1), (1, 1)]]
CENTRE = (0, 0)
TURNS = [(2, 0), (1, 0), (2, 1), (1, 0), (2, 0), (2, 1), (1, 0), (2, 0), (1, 0), (2, 1), (2, 0), (1, 1),
         (2, 0), (2, 1), (1, 1), (2, 0), (1, 1), (2, 0), (1, 1), (2, 1), (1, 1), (2, 1), (2, 1)]
SIDE = (1, 1)
MIX_TAPS = [(dy, dx) for dy in (-1, 0, 1) for dx in (-1, 0, 1) if (dy, dx) not in (CENTRE, SIDE)]


def build(nc: bass.Bass, x, params, w1_t, w2_t, fc1_t, fc2_t, out):
    f32, f32r = mybir.dt.float32, mybir.dt.float32r
    ACT, ALU = mybir.ActivationFunctionType, mybir.AluOpType

    with ExitStack() as ctx:
        def sb(name, shape, dt=f32):
            return ctx.enter_context(nc.sbuf_tensor(name, shape, dt))

        def sem(name):
            return ctx.enter_context(nc.semaphore(name))

        xring = sb("xring", [P, 2, CHUNKS, HEIGHT * WIDTH])
        split_size = (ROWS + 1) * PITCH + 3
        xhi = sb("xhi", [P, 2, CHUNKS, split_size], f32r)
        xlo = sb("xlo", [P, 2, CHUNKS, split_size], f32r)
        mix_size = (HEIGHT + 2) * PITCH + 2
        mix = sb("mix", [P, CHUNKS, mix_size])
        edge = sb("edge", [P, SIZE])
        ehi = sb("ehi", [P, CHUNKS, SIZE], f32r)
        elo = sb("elo", [P, CHUNKS, SIZE], f32r)
        acc2 = sb("acc2", [P, CHUNKS, SIZE])
        y = sb("y", [P, CHUNKS, SIZE])
        yhi = sb("yhi", [P, CHUNKS, SIZE], f32r)
        ylo = sb("ylo", [P, CHUNKS, SIZE], f32r)
        side = sb("side", [P, SIZE])
        w1x_att = sb("w1x_att", [P, CHUNKS, CHANNELS])
        unused = w1x_att[:].rearrange("p k o -> p (k o)").bitcast(mybir.dt.bfloat16)
        gain = sb("gain", [P, SIZE])
        w1x = sb("w1x", [P, CHUNKS, CHANNELS])
        w1x_hi = sb("w1x_hi", [P, CHUNKS, CHANNELS], f32r)
        w1x_lo = sb("w1x_lo", [P, CHUNKS, CHANNELS], f32r)
        w1e_hi = sb("w1e_hi", [P, CHUNKS, CHANNELS], f32r)
        w1e_lo = sb("w1e_lo", [P, CHUNKS, CHANNELS], f32r)
        w2_hi = sb("w2_hi", [P, CHUNKS, CHANNELS], f32r)
        w2_lo = sb("w2_lo", [P, CHUNKS, CHANNELS], f32r)
        diag_hi = sb("diag_hi", [P, sum(map(len, PE_TAPS)), P], f32r)
        diag_lo = sb("diag_lo", [P, sum(map(len, PE_TAPS)), P], f32r)
        prm = sb("prm", [P, PARAMS])
        tap_hi = sb("tap_hi", [P, 9 * CHUNKS], f32r)
        tap_lo = sb("tap_lo", [P, 9 * CHUNKS])
        bn = sb("bn", [P, 4, 6])
        fc1 = sb("fc1", [P, CHUNKS, HIDDEN])
        fc2 = sb("fc2", [HIDDEN, CHANNELS])
        sums = sb("sums", [P, 2, CHUNKS, STRIPS])
        hidden = sb("hidden", [HIDDEN, 1])
        att = sb("att", [P, CHUNKS])
        w1e_raw = y[:, 1, 0:2 * CHANNELS].rearrange("p (k o) -> p k o", k=CHUNKS)
        w2_raw = y[:, 1, 2 * CHANNELS:4 * CHANNELS].rearrange("p (k o) -> p k o", k=CHUNKS)
        ident = gain[:, 0:P]

        acc1 = ctx.enter_context(nc.psum_tensor("acc1", [P, CHUNKS, SIZE], f32))
        prod = ctx.enter_context(nc.psum_tensor("prod", [P, 4, HALF], f32))

        x_loaded = [[sem(f"x_loaded{i}_{c}") for c in range(CHUNKS)] for i in range(RING)]
        x_stored = sem("x_stored")
        params_loaded, weights_loaded = sem("params_loaded"), sem("weights_loaded")
        att_weights_loaded = sem("att_weights_loaded")
        pads_zeroed, ident_ready = sem("pads_zeroed"), sem("ident_ready")
        setup_step, root_ready = sem("setup_step"), sem("root_ready")
        tap_hi_ready, his_ready = sem("tap_hi_ready"), sem("his_ready")
        diags_ready, weights_ready = sem("diags_ready"), sem("weights_ready")
        x_summed = sem("x_summed")
        xhi_ready, xlo_ready = sem("xhi_ready"), sem("xlo_ready")
        taps_on_pe = sem("taps_on_pe")
        acc1_tap = [sem(f"acc1_tap{c}") for c in range(CHUNKS)]
        edge_ready = sem("edge_ready")
        ehi_ready, elo_ready = sem("ehi_ready"), sem("elo_ready")
        w1_done, w2_done = sem("w1_done"), sem("w2_done")
        mix_ready = [sem(f"mix_ready{c}") for c in range(CHUNKS)]
        acc2_begun = sem("acc2_begun")
        acc2_tap = [sem(f"acc2_tap{c}") for c in range(CHUNKS)]
        side_ready, y_summed = sem("side_ready"), sem("y_summed")
        yhi_ready, ylo_ready = sem("yhi_ready"), sem("ylo_ready")
        gain_ready = [sem(f"gain_ready{c}") for c in range(CHUNKS)]
        out_ready = sem("out_ready")
        fc1_done, hidden_ready = sem("fc1_done"), sem("hidden_ready")
        fc2_done, att_ready = sem("fc2_done"), sem("att_ready")
        w1x_att_ready = sem("w1x_att_ready")
        w1x_hi_ready, w1x_lo_ready = sem("w1x_hi_ready"), sem("w1x_lo_ready")

        block = ctx.enter_context(nc.Block())

        def exists(pair, k):
            return not isinstance(pair, int) or 0 <= pair * RING + k < TOTAL

        def count(per_strip, pair, k, extra=0):
            return pair * (RING * per_strip) + (k * per_strip + extra)

        def image_count(per_image, pair, k, extra):
            return pair * (2 * per_image) + (k // STRIPS * per_image + extra)

        def min_count(per_strip, pair, k):
            return count(per_strip, pair, k) if exists(pair, k - 1) else per_strip * TOTAL

        def turns(pair, k):
            return pair * 16 + 16 * (k // RING + 1)

        def first(k):
            return k % STRIPS == 0

        def last(k):
            return k % STRIPS == STRIPS - 1

        def tap_of(conv, tap, c):
            dy, dx = tap
            return TAPS + (conv * 9 + (dy + 1) * 3 + dx + 1) * CHUNKS + c

        def x_rows(k, c, row, rows, col=0, cols=WIDTH):
            at = (k % STRIPS) * ROWS + row
            image = xring[:, (k // STRIPS) % 2, c, at * WIDTH:(at + rows) * WIDTH]
            return image.rearrange("p (r w) -> p r w", w=WIDTH)[:, :, col:col + cols]

        def padded(row_tile, row, rows, dx=0):
            at = row * PITCH + 1 + dx
            return row_tile[:, at:at + rows * PITCH].rearrange("p (r w) -> p r w", w=PITCH)[:, :, 0:WIDTH]

        def written(row_tile, row, rows):
            return padded(row_tile, row, rows)

        def steps(eng, step, begin):
            for k in range(begin, 4):
                step(0, k)
            with eng.Fori(0, PAIRS - 1) as pair:
                for k in range(4, 4 + RING):
                    step(pair, k)
            for k in range(4, 4 + RING):
                step(PAIRS - 1, k)

        x_pairs, out_pairs = (t.rearrange("(n i) (k p) h w -> n i p k (h w)", i=2, p=P) for t in (x, out))

        def load(sp, pair, slot, c):
            i, at = slot // STRIPS, (slot % STRIPS) * SIZE
            sp.dma_start(xring[:, i, c, at:at + SIZE], x_pairs[pair, i, :, c, at:at + SIZE]
                         ).then_inc(x_loaded[slot][c], 16)

        def store(sp, pair, slot, c):
            sp.wait_ge(out_ready, count(2, pair, slot, c + 1))
            i, at = slot // STRIPS, (slot % STRIPS) * SIZE
            sp.dma_start(out_pairs[pair, i, :, c, at:at + SIZE], xring[:, i, c, at:at + SIZE]
                         ).then_inc(x_stored, 16)

        @block.sync
        def _(sp):
            sp.dma_start(prm[:], params).then_inc(params_loaded, 16)
            for c in range(CHUNKS):
                load(sp, 0, 0, c)
                load(sp, 0, 1, c)
            sp.dma_start(w1e_raw, w1_t[:, CHUNKS:2 * CHUNKS, :]).then_inc(weights_loaded, 16)
            sp.dma_start(w2_raw, w2_t).then_inc(weights_loaded, 16)
            sp.dma_start(w1x[:], w1_t[:, 0:CHUNKS, :]).then_inc(att_weights_loaded, 16)
            sp.dma_start(fc1[:], fc1_t).then_inc(att_weights_loaded, 16)
            sp.dma_start(fc2[:], fc2_t).then_inc(att_weights_loaded, 16)
            for slot in range(2, RING):
                for c in range(CHUNKS):
                    load(sp, 0, slot, c)
            with sp.Fori(0, PAIRS - 1) as pair:
                for slot in range(RING):
                    for c in range(CHUNKS):
                        store(sp, pair, slot, c)
                        sp.wait_ge(x_stored, count(32, pair, slot, 16 * (c + 1)))
                        load(sp, pair + 1, slot, c)
            for slot in range(RING):
                for c in range(CHUNKS):
                    store(sp, PAIRS - 1, slot, c)
            sp.wait_ge(x_stored, 32 * TOTAL)

        @block.tensor
        def _(pe):
            pe.wait_ge(pads_zeroed, 1)
            pe.wait_ge(diags_ready, 1)

            def conv_taps(pair, k, c, half):
                buf = k % 2
                jobs = [(w, v) for w, v in ((diag_hi, xhi), (diag_lo, xhi), (diag_hi, xlo))]
                for job, (w, v) in enumerate(jobs):
                    if half == 0 and job == 0:
                        pe.wait_ge(xhi_ready, count(2, pair, k, c + 1))
                    if half == 0 and job == 2:
                        pe.wait_ge(xlo_ready, count(2, pair, k, c + 1))
                    for t, (dy, dx) in enumerate(PE_TAPS[c]):
                        rows = HALF_ROWS - (last(k) and half == 1 and dy == 1)
                        at = half * HALF
                        mm = nc.tensor.matmul(
                            acc1[:, c, at:at + rows * WIDTH], w[:, c * len(PE_TAPS[0]) + t, :],
                            padded(v[:, buf, c, :], half * HALF_ROWS + dy, rows, dx),
                            start=(job == 0 and t == 0), stop=(job == 2 and t == len(PE_TAPS[c]) - 1))
                return mm

            def step(pair, k):
                conv, image = exists(pair, k + 1), exists(pair, k) and first(k)
                if conv:
                    if exists(pair, k):
                        pe.wait_ge(edge_ready, count(2, pair, k, 1))
                    conv_taps(pair, k + 1, 0, 0)
                if image:
                    if isinstance(pair, int) and pair == 0 and k == 0:
                        pe.wait_ge(att_weights_loaded, 3 * 16)
                    pe.wait_ge(x_summed, count(2, pair, k, 2 * STRIPS))
                    if exists(pair, k - 4):
                        pe.wait_ge(gain_ready[0], count(2, pair, k - 4, 1))
                    for n in range(CHUNKS * STRIPS):
                        c, s = n // STRIPS, n % STRIPS
                        mm = nc.tensor.matmul(prod[0:HIDDEN, 0, 0:1], fc1[:, c, :],
                                              sums[:, (k // STRIPS) % 2, c, s:s + 1],
                                              start=(n == 0), stop=(n == CHUNKS * STRIPS - 1))
                    mm.then_inc(fc1_done, 1)
                if conv:
                    conv_taps(pair, k + 1, 0, 1).then_inc(taps_on_pe, 1)
                if image:
                    pe.wait_ge(hidden_ready, image_count(1, pair, k, 1))
                    if exists(pair, k - 4):
                        pe.wait_ge(gain_ready[0], count(2, pair, k - 4, 2))
                    for c in range(CHUNKS):
                        mm = nc.tensor.matmul(prod[:, 1, c:c + 1], fc2[:, c * P:(c + 1) * P],
                                              hidden[:], start=True, stop=True)
                    mm.then_inc(fc2_done, 1)
                if conv:
                    if exists(pair, k):
                        pe.wait_ge(edge_ready, count(2, pair, k, 2))
                    conv_taps(pair, k + 1, 1, 0)
                    conv_taps(pair, k + 1, 1, 1).then_inc(taps_on_pe, 1)

                if isinstance(pair, int) and pair == 0 and k == 0:
                    pe.wait_ge(weights_ready, 1)
                if exists(pair, k):
                    buf = k % 2
                    for u in range(4):
                        o, half = u // 2, u % 2
                        if u == 0:
                            pe.wait_ge(w1x_hi_ready, image_count(1, pair, k, 1))
                            if first(k):
                                pe.wait_ge(att_ready, image_count(1, pair, k, 1))
                        if exists(pair, k - 4):
                            pe.wait_ge(gain_ready[o], count(2, pair, k - 4, half + 1))
                        jobs = []
                        for cc in range(CHUNKS):
                            v, l = (padded(b[:, buf, cc, :], half * HALF_ROWS, HALF_ROWS) for b in (xhi, xlo))
                            jobs += [(w1x_hi, cc, v, None), (w1x_hi, cc, l, None), (w1x_lo, cc, v, "att")]
                        for cc in range(CHUNKS):
                            v, l = (b[:, cc, half * HALF:(half + 1) * HALF] for b in (ehi, elo))
                            jobs += [(w1e_hi, cc, v, "ehi"), (w1e_lo, cc, v, None), (w1e_hi, cc, l, "elo")]
                        for n, (w, cc, v, needs) in enumerate(jobs):
                            if u == 0 and needs == "att":
                                pe.wait_ge(w1x_lo_ready, image_count(1, pair, k, 1))
                            if u == 0 and needs == "ehi":
                                pe.wait_ge(ehi_ready, count(2, pair, k, cc + 1))
                            if u == 0 and needs == "elo":
                                pe.wait_ge(elo_ready, count(2, pair, k, cc + 1))
                            mm = nc.tensor.matmul(prod[:, u, :], w[:, cc, o * P:(o + 1) * P], v,
                                                  start=(n == 0), stop=(n == len(jobs) - 1))
                        mm.then_inc(w1_done, 1)

                if exists(pair, k - 3):
                    for u in range(4):
                        o, half = u // 2, u % 2
                        if exists(pair, k):
                            pe.wait_ge(mix_ready[o], count(2, pair, k, half + 1))
                        else:
                            pe.wait_ge(gain_ready[o], count(2, pair, k - 4, half + 1))
                        jobs = []
                        for cc in range(CHUNKS):
                            v, l = (b[:, cc, half * HALF:(half + 1) * HALF] for b in (yhi, ylo))
                            jobs += [(w2_hi, cc, v, "yhi"), (w2_lo, cc, v, None), (w2_hi, cc, l, "ylo")]
                        for n, (w, cc, v, needs) in enumerate(jobs):
                            if u == 0 and needs == "yhi":
                                pe.wait_ge(yhi_ready, count(2, pair, k - 3, cc + 1))
                            if u == 0 and needs == "ylo":
                                pe.wait_ge(ylo_ready, count(2, pair, k - 3, cc + 1))
                            mm = nc.tensor.matmul(prod[:, u, :], w[:, cc, o * P:(o + 1) * P], v,
                                                  start=(n == 0), stop=(n == len(jobs) - 1))
                        mm.then_inc(w2_done, 1)

            steps(pe, step, -1)

        @block.scalar
        def _(act):
            act.wait_ge(setup_step, 1)
            nc.scalar.activation(bn[:, 3, :], bn[:, 2, :], ACT.Sqrt).then_inc(root_ready, 1)
            act.wait_ge(params_loaded, 16)
            nc.scalar.activation(tap_hi[:], prm[:, TAPS:TAPS + 9 * CHUNKS], ACT.Copy).then_inc(tap_hi_ready, 1)
            act.wait_ge(pads_zeroed, 1)

            def sum_x(pair, k, c):
                if exists(pair, k - 4):
                    act.wait_ge(w1x_lo_ready, image_count(1, pair, k - 4, 1))
                act.wait_ge(x_loaded[k % RING][c], turns(pair, k))
                if exists(pair, k - 1) or c:
                    act.wait_ge(x_summed, count(2, pair, k, c))
                nc.scalar.activation(unused.rearrange("p (r w) -> p r w", w=WIDTH),
                                     x_rows(k, c, 0, ROWS), ACT.Copy,
                                     accum_out=sums[:, (k // STRIPS) % 2, c, k % STRIPS:k % STRIPS + 1]
                                     ).then_inc(x_summed, 1)

            def round_x(pair, k, c):
                act.wait_ge(x_loaded[k % RING][c], turns(pair, k))
                if not last(k):
                    act.wait_ge(x_loaded[(k + 1) % RING][c], turns(pair, k + 1))
                if c == 0 and exists(pair, k - 2):
                    act.wait_ge(w1_done, count(4, pair, k - 2, 4))
                rows = ROWS + (not last(k))
                nc.scalar.activation(written(xhi[:, k % 2, c, :], 0, rows), x_rows(k, c, 0, rows),
                                     ACT.Copy).then_inc(xhi_ready, 1)

            def edge_out(pair, k, c):
                act.wait_ge(acc1_tap[c], count(len(DVE_TAPS[c]), pair, k + 1))
                if exists(pair, k - 1) or c:
                    act.wait_ge(ehi_ready, count(2, pair, k, c))
                    act.wait_ge(elo_ready, count(2, pair, k, c))
                if isinstance(pair, int) and pair == 0 and k == 0 and c == 0:
                    act.wait_ge(diags_ready, 1)
                nc.scalar.activation(edge[:], acc1[:, c, :], ACT.Relu, bias=bn[:, 1, c:c + 1],
                                     scale=bn[:, 0, c:c + 1]).then_inc(edge_ready, 1)

            def round_edge(pair, k, c):
                act.wait_ge(edge_ready, count(2, pair, k, c + 1))
                if exists(pair, k - 1):
                    act.wait_ge(w1_done, count(4, pair, k))
                nc.scalar.activation(ehi[:, c, :], edge[:], ACT.Copy).then_inc(ehi_ready, 1)

            def mix_out(pair, k, u):
                o, half = u // 2, u % 2
                act.wait_ge(w1_done, count(4, pair, k, u + 1))
                if exists(pair, k - 3):
                    act.wait_ge(acc2_tap[o], count(len(MIX_TAPS), pair, k - 2))
                rows = written(mix[:, o, :], 1 + (k % STRIPS) * ROWS + half * HALF_ROWS, HALF_ROWS)
                nc.scalar.activation(rows, prod[:, u, :].rearrange("p (r w) -> p r w", w=WIDTH),
                                     ACT.Identity, bias=bn[:, 1, 2 + o:3 + o],
                                     scale=bn[:, 0, 2 + o:3 + o]).then_inc(mix_ready[o], 1)

            def begin_acc2(pair, k, c):
                act.wait_ge(mix_ready[c], count(2, pair, k, 2))
                if exists(pair, k - 1):
                    act.wait_ge(acc2_tap[c], count(len(MIX_TAPS), pair, k))
                at = tap_of(1, CENTRE, c)
                nc.scalar.activation(acc2[:, c, :].rearrange("p (r w) -> p r w", w=WIDTH),
                                     padded(mix[:, c, :], 1 + (k % STRIPS) * ROWS, ROWS),
                                     ACT.Copy, scale=prm[:, at:at + 1]).then_inc(acc2_begun, 1)

            def side_out(pair, k, c):
                if last(k):
                    act.wait_ge(mix_ready[c], count(2, pair, k, 2))
                else:
                    act.wait_ge(mix_ready[c], count(2, pair, k + 1, 1))
                if exists(pair, k - 1) or c:
                    act.wait_ge(y_summed, count(2, pair, k, c))
                at = tap_of(1, SIDE, c)
                nc.scalar.activation(side[:].rearrange("p (r w) -> p r w", w=WIDTH),
                                     padded(mix[:, c, :], 1 + (k % STRIPS) * ROWS + SIDE[0], ROWS, SIDE[1]),
                                     ACT.Copy, scale=prm[:, at:at + 1]).then_inc(side_ready, 1)

            def round_y(pair, k, c):
                act.wait_ge(y_summed, count(2, pair, k, c + 1))
                if exists(pair, k - 1):
                    act.wait_ge(w2_done, count(4, pair, k))
                nc.scalar.activation(yhi[:, c, :], y[:, c, :], ACT.Copy).then_inc(yhi_ready, 1)

            def gain_out(pair, k, u):
                o, half = u // 2, u % 2
                act.wait_ge(w2_done, count(4, pair, k, u + 1))
                if exists(pair, k - 1) or o:
                    act.wait_ge(out_ready, count(2, pair, k, o))
                nc.scalar.activation(gain[:, half * HALF:(half + 1) * HALF], prod[:, u, :],
                                     ACT.Identity, bias=bn[:, 1, 4 + o:5 + o],
                                     scale=bn[:, 0, 4 + o:5 + o]).then_inc(gain_ready[o], 1)

            def hide(pair, k):
                act.wait_ge(fc1_done, image_count(1, pair, k, 1))
                nc.scalar.activation(hidden[:], prod[0:HIDDEN, 0, 0:1], ACT.Relu,
                                     scale=1.0 / (HEIGHT * WIDTH)).then_inc(hidden_ready, 1)

            def attend(pair, k):
                act.wait_ge(fc2_done, image_count(1, pair, k, 1))
                nc.scalar.activation(att[:], prod[:, 1, 0:CHUNKS], ACT.Sigmoid).then_inc(att_ready, 1)
                act.wait_ge(att_ready, image_count(1, pair, k, 1))
                if isinstance(pair, int) and pair == 0 and k == 0:
                    act.wait_ge(att_weights_loaded, 3 * 16)
                act.wait_ge(x_summed, min_count(2, pair, k + 4))
                for c in range(CHUNKS):
                    nc.scalar.activation(w1x_att[:, c, :], w1x[:, c, :], ACT.Copy,
                                         scale=att[:, c:c + 1]).then_inc(w1x_att_ready, 1)
                if exists(pair, k - 1):
                    act.wait_ge(w1_done, count(4, pair, k))
                act.wait_ge(w1x_att_ready, image_count(2, pair, k, 2))
                nc.scalar.activation(w1x_hi[:], w1x_att[:], ACT.Copy).then_inc(w1x_hi_ready, 1)

            def step(pair, k):
                now, y_next, gain_now = exists(pair, k), exists(pair, k - 2), exists(pair, k - 3)
                sum_now = exists(pair, k + 3) and not last(k + 3)
                if y_next:
                    begin_acc2(pair, k - 2, 0)
                if now and first(k):
                    hide(pair, k)
                if now:
                    edge_out(pair, k, 1)
                    round_edge(pair, k, 1)
                if y_next:
                    begin_acc2(pair, k - 2, 1)
                if now and first(k):
                    attend(pair, k)
                if gain_now:
                    side_out(pair, k - 3, 1)
                    round_y(pair, k - 3, 0)
                if exists(pair, k - 4):
                    gain_out(pair, k - 4, 2)
                    gain_out(pair, k - 4, 3)
                if sum_now:
                    sum_x(pair, k + 3, 0)
                if gain_now:
                    round_y(pair, k - 3, 1)
                if now:
                    mix_out(pair, k, 0)
                if y_next:
                    side_out(pair, k - 2, 0)
                if now:
                    mix_out(pair, k, 1)
                if exists(pair, k + 1):
                    edge_out(pair, k + 1, 0)
                if now:
                    mix_out(pair, k, 2)
                if sum_now:
                    sum_x(pair, k + 3, 1)
                if exists(pair, k + 2):
                    round_x(pair, k + 2, 0)
                if now:
                    mix_out(pair, k, 3)
                if exists(pair, k + 2):
                    round_x(pair, k + 2, 1)
                if exists(pair, k + 1):
                    round_edge(pair, k + 1, 0)
                if gain_now:
                    gain_out(pair, k - 3, 0)
                    gain_out(pair, k - 3, 1)
                if last(k) and exists(pair, k + 4):
                    for c in range(CHUNKS):
                        sum_x(pair, k + 4, c)

            for c in range(CHUNKS):
                round_x(0, 0, c)
            act.wait_ge(weights_loaded, 2 * 16)
            nc.scalar.activation(w1e_hi[:], w1e_raw, ACT.Copy).then_inc(his_ready, 1)
            nc.scalar.activation(w2_hi[:], w2_raw, ACT.Copy).then_inc(his_ready, 1)
            for c in range(CHUNKS):
                round_x(0, 1, c)
            for k in range(STRIPS - 1):
                for c in range(CHUNKS):
                    sum_x(0, k, c)
            edge_out(0, 0, 0)
            round_edge(0, 0, 0)
            for c in range(CHUNKS):
                sum_x(0, STRIPS - 1, c)
            steps(act, step, 0)

        @block.vector
        def _(dve):
            made = [0]

            def link(ins):
                made[0] += 1
                ins.then_inc(setup_step, 1)
                dve.wait_ge(setup_step, made[0])

            scale, shift, v, r = (bn[:, n, :] for n in range(4))
            t = y[:, 0, 0:6]
            dve.wait_ge(params_loaded, 16)
            link(nc.vector.tensor_scalar(v, prm[:, VAR:VAR + 6], EPS, None, ALU.add))
            link(nc.vector.tensor_tensor(prm[:, MEAN + 2:MEAN + 6], prm[:, MEAN + 2:MEAN + 6],
                                         prm[:, BIAS:BIAS + 4], ALU.subtract))
            dve.wait_ge(root_ready, 1)
            link(nc.vector.reciprocal(r, r))
            link(nc.vector.tensor_tensor(t, r, r, ALU.mult))
            link(nc.vector.tensor_tensor(t, t, v, ALU.mult))
            link(nc.vector.tensor_scalar(t, t, -0.5, 1.5, ALU.mult, ALU.add))
            link(nc.vector.tensor_tensor(r, r, t, ALU.mult))
            link(nc.vector.tensor_tensor(scale, r, prm[:, GAMMA:GAMMA + 6], ALU.mult))
            link(nc.vector.tensor_tensor(t, scale, prm[:, MEAN:MEAN + 6], ALU.mult))
            link(nc.vector.tensor_tensor(shift, prm[:, BETA:BETA + 6], t, ALU.subtract))
            dve.wait_ge(tap_hi_ready, 1)
            link(nc.vector.tensor_tensor(tap_lo[:], prm[:, TAPS:TAPS + 9 * CHUNKS], tap_hi[:].bitcast(f32),
                                         ALU.subtract))
            dve.wait_ge(ident_ready, 2)
            for n, (c, tap) in enumerate((c, tap) for c in range(CHUNKS) for tap in PE_TAPS[c]):
                at = tap_of(0, tap, c) - TAPS
                nc.vector.tensor_scalar(diag_hi[:, n, :], ident, tap_hi[:, at:at + 1].bitcast(f32),
                                        None, ALU.mult)
                made_last = nc.vector.tensor_scalar(diag_lo[:, n, :], ident, tap_lo[:, at:at + 1],
                                                    None, ALU.mult)
            made_last.then_inc(diags_ready, 1)
            dve.wait_ge(his_ready, 2)
            nc.vector.tensor_tensor(w1e_lo[:], w1e_raw, w1e_hi[:].bitcast(f32), ALU.subtract)
            nc.vector.tensor_tensor(w2_lo[:], w2_raw, w2_hi[:].bitcast(f32), ALU.subtract
                                    ).then_inc(weights_ready, 1)

            def acc1_op(pair, k, c, n):
                if n == 0:
                    dve.wait_ge(taps_on_pe, count(2, pair, k, c + 1))
                else:
                    dve.wait_ge(acc1_tap[c], count(len(DVE_TAPS[c]), pair, k, n))
                dy, dx = DVE_TAPS[c][n]
                top = 1 if first(k) and dy < 0 else 0
                rows = ROWS - top - (1 if last(k) and dy > 0 else 0)
                col, cols = max(0, -dx), WIDTH - abs(dx)
                acc = acc1[:, c, top * WIDTH:(top + rows) * WIDTH].rearrange("p (r w) -> p r w", w=WIDTH)
                acc = acc[:, :, col:col + cols]
                at = tap_of(0, (dy, dx), c)
                nc.vector.scalar_tensor_tensor(
                    out=acc, in0=x_rows(k, c, top + dy, rows, col + dx, cols), scalar=prm[:, at:at + 1],
                    in1=acc, op0=ALU.mult, op1=ALU.add).then_inc(acc1_tap[c], 1)

            def acc2_op(pair, k, c, n):
                if n == 0:
                    dve.wait_ge(acc2_begun, count(2, pair, k, c + 1))
                    if not last(k):
                        dve.wait_ge(mix_ready[c], count(2, pair, k + 1, 1))
                else:
                    dve.wait_ge(acc2_tap[c], count(len(MIX_TAPS), pair, k, n))
                final = n == len(MIX_TAPS) - 1
                if final and exists(pair, k - 1):
                    dve.wait_ge(yhi_ready, count(2, pair, k - 1, c + 1))
                    dve.wait_ge(ylo_ready, count(2, pair, k - 1, c + 1))
                acc = acc2[:, c, :].rearrange("p (r w) -> p r w", w=WIDTH)
                to = y[:, c, :].rearrange("p (r w) -> p r w", w=WIDTH) if final else acc
                dy, dx = MIX_TAPS[n]
                at = tap_of(1, (dy, dx), c)
                nc.vector.scalar_tensor_tensor(
                    out=to, in0=padded(mix[:, c, :], 1 + (k % STRIPS) * ROWS + dy, ROWS, dx),
                    scalar=prm[:, at:at + 1], in1=acc, op0=ALU.mult, op1=ALU.add).then_inc(acc2_tap[c], 1)

            def step(pair, k):
                taps = {turn: 0 for turn in TURNS}
                for conv, c in TURNS:
                    if conv == 1 and exists(pair, k + 1):
                        acc1_op(pair, k + 1, c, taps[conv, c])
                    if conv == 2 and exists(pair, k - 2):
                        acc2_op(pair, k - 2, c, taps[conv, c])
                    taps[conv, c] += 1

            steps(dve, step, -1)

        @block.gpsimd
        def _(pool):
            pool.memset(ident, 0.0).then_inc(ident_ready, 1)
            pool.wait_ge(ident_ready, 1)
            pool.affine_select(out=ident, in_=ident, compare_op=ALU.not_equal, fill=1.0, base=0,
                               pattern=[[-1, P]], channel_multiplier=1).then_inc(ident_ready, 1)
            for c in range(CHUNKS):
                for buf in range(2):
                    for tile in (xhi, xlo):
                        pool.memset(tile[:, buf, c, 0:(ROWS + 1) * PITCH + 1:PITCH].bitcast(f32), 0.0)
                pool.memset(mix[:, c, 0:PITCH + 1], 0.0)
                pool.memset(mix[:, c, 2 * PITCH:(HEIGHT + 1) * PITCH:PITCH], 0.0)
                zeroed = pool.memset(mix[:, c, (HEIGHT + 1) * PITCH:mix_size], 0.0)
            zeroed.then_inc(pads_zeroed, 1)

            def rest_of_x(pair, k, c):
                pool.wait_ge(xhi_ready, count(2, pair, k, c + 1))
                rows = ROWS + (not last(k))
                nc.gpsimd.tensor_tensor(written(xlo[:, k % 2, c, :], 0, rows), x_rows(k, c, 0, rows),
                                        written(xhi[:, k % 2, c, :], 0, rows).bitcast(f32), ALU.subtract
                                        ).then_inc(xlo_ready, 1)

            def rest_of_edge(pair, k, c):
                pool.wait_ge(ehi_ready, count(2, pair, k, c + 1))
                nc.gpsimd.tensor_tensor(elo[:, c, :], edge[:], ehi[:, c, :].bitcast(f32), ALU.subtract
                                        ).then_inc(elo_ready, 1)

            def rest_of_y(pair, k, c):
                pool.wait_ge(yhi_ready, count(2, pair, k, c + 1))
                nc.gpsimd.tensor_tensor(ylo[:, c, :], y[:, c, :], yhi[:, c, :].bitcast(f32), ALU.subtract
                                        ).then_inc(ylo_ready, 1)

            def add_side(pair, k, c):
                pool.wait_ge(acc2_tap[c], count(len(MIX_TAPS), pair, k + 1))
                pool.wait_ge(side_ready, count(2, pair, k, c + 1))
                nc.gpsimd.tensor_tensor(y[:, c, :], y[:, c, :], side[:], ALU.add).then_inc(y_summed, 1)

            def rest_of_w1x(pair, k):
                pool.wait_ge(w1x_hi_ready, image_count(1, pair, k, 1))
                nc.gpsimd.tensor_tensor(w1x_lo[:], w1x_att[:], w1x_hi[:].bitcast(f32), ALU.subtract
                                        ).then_inc(w1x_lo_ready, 1)

            def times_x(pair, k, c):
                pool.wait_ge(gain_ready[c], count(2, pair, k, 2))
                at = (k % STRIPS) * SIZE
                strip = xring[:, (k // STRIPS) % 2, c, at:at + SIZE]
                nc.gpsimd.tensor_tensor(strip, strip, gain[:], ALU.mult).then_inc(out_ready, 1)

            def step(pair, k):
                if exists(pair, k):
                    rest_of_edge(pair, k, 1)
                    if first(k):
                        rest_of_w1x(pair, k)
                if exists(pair, k - 4):
                    times_x(pair, k - 4, 0)
                if exists(pair, k - 3):
                    add_side(pair, k - 3, 1)
                if exists(pair, k - 4):
                    times_x(pair, k - 4, 1)
                if exists(pair, k - 3):
                    rest_of_y(pair, k - 3, 0)
                    rest_of_y(pair, k - 3, 1)
                if exists(pair, k + 2):
                    rest_of_x(pair, k + 2, 0)
                    rest_of_x(pair, k + 2, 1)
                if exists(pair, k + 1):
                    rest_of_edge(pair, k + 1, 0)
                if exists(pair, k - 2):
                    add_side(pair, k - 2, 0)

            steps(pool, step, -2)


def kernel(**inputs):
    import numpy as _np
    import concourse.bacc as _bacc
    from concourse import mybir as _mybir
    from concourse.bass_utils import run_bass_kernel_spmd as _run

    a = {n.removeprefix("L0_conv_"): _np.asarray(v) for n, v in inputs.items()}

    def on_partitions(v):
        return v.reshape(CHUNKS, P, -1).transpose(1, 0, 2)

    names = [f"{b}_{f}" for f in ("gamma", "beta", "mean", "var") for b in ("edge", "bn1", "bn2")]
    columns = [a[n].reshape(CHANNELS, 1) for n in names + ["fusion_b", "balance_b"]]
    columns += [a[n].reshape(CHANNELS, 9) for n in ("edge_w", "deform_w")]
    laid = {
        "x": a["x"],
        "params": on_partitions(_np.concatenate(columns, axis=1)).transpose(0, 2, 1).reshape(P, -1),
        "w1_t": a["fusion_w"].T.reshape(2 * CHUNKS, P, CHANNELS).transpose(1, 0, 2),
        "w2_t": on_partitions(a["balance_w"].T),
        "fc1_t": on_partitions(a["fc1_w"].T),
        "fc2_t": a["fc2_w"].T,
    }
    nc = _bacc.Bacc("TRN2", target_bir_lowering=False, num_devices=1,
                    dynamic_dma_scratch_size=1024)
    arrays, args = {}, []
    for name, v in laid.items():
        v = _np.ascontiguousarray(v)
        arrays[f"in_{name}"] = v
        args.append(nc.dram_tensor(f"in_{name}", v.shape, _mybir.dt.from_np(v.dtype), kind="ExternalInput").ap())
    shape = (IMAGES, CHANNELS, HEIGHT, WIDTH)
    args.append(nc.dram_tensor("out_0", shape, _mybir.dt.float32, kind="ExternalOutput").ap())
    build(nc, *args)
    return _run(nc, [arrays], core_ids=[0]).results[0]["out_0"]
```
